# Optimizing a Trainium2 kernel written in Bass

```python
import numpy as np
import jax
import jax.numpy as jnp

def _softmax(x, axis=-1):
    return jax.nn.softmax(x, axis=axis)

def _gelu(x):
    return jax.nn.gelu(x, approximate=True)

def _silu(x):
    return jax.nn.silu(x)

def _sigmoid(x):
    return jax.nn.sigmoid(x)

def _layernorm(x, axis=-1, eps=1e-05):
    m = jnp.mean(x, axis=axis, keepdims=True)
    v = jnp.var(x, axis=axis, keepdims=True)
    return (x - m) / jnp.sqrt(v + eps)

def _scatter_add(tgt, idx, src, axis=0):
    return tgt.at[idx].add(src)

def _segment_sum(src, seg, n):
    return jax.ops.segment_sum(src, seg, n)
kernel_name = 'mk_seq_postln_d1_jaxref_r8_9b6055'

def setup_inputs(seed: int=0):
    np.random.seed(seed)
    _w = jnp.asarray

    def _L0_attn_setup():
        import jax, jax.numpy as jnp
        import numpy as np
        import math
        NUM_HEADS = 16
        TPMS_WEIGHT = 0.3
        TWO_PI = 2.0 * math.pi

        def _tpms_mask(L, phase, threshold, temperature):
            pos = jnp.arange(L, dtype=jnp.float32) / L * TWO_PI
            pq = pos[None, :, None] + phase[:, 0][:, None, None]
            pk = pos[None, None, :] + phase[:, 1][:, None, None]
            pz = (pos[None, :, None] + pos[None, None, :]) * 0.5 + phase[:, 2][:, None, None]
            t = jax.lax.stop_gradient(threshold)
            val = jnp.sin(pq) * jnp.cos(pk) + jnp.sin(pk) * jnp.cos(pz) + jnp.sin(pz) * jnp.cos(pq) - t
            return jax.nn.sigmoid(val / (temperature + 1e-06))
        key = jax.random.key(seed)
        ks = jax.random.split(key, 8)
        B, L, H = (2, 256, 128)
        nh = NUM_HEADS
        std = 0.02
        x = jax.random.normal(ks[0], (B, L, H), dtype=jnp.float32)
        Wq = jax.random.normal(ks[1], (H, H), dtype=jnp.float32) * std
        Wk = jax.random.normal(ks[2], (H, H), dtype=jnp.float32) * std
        Wv = jax.random.normal(ks[3], (H, H), dtype=jnp.float32) * std
        Wo = jax.random.normal(ks[4], (H, H), dtype=jnp.float32) * std
        bq = jnp.zeros((H,), jnp.float32)
        bk = jnp.zeros((H,), jnp.float32)
        bv = jnp.zeros((H,), jnp.float32)
        bo = jnp.zeros((H,), jnp.float32)
        phase = jax.random.normal(ks[5], (nh, 3), dtype=jnp.float32) * 0.5
        threshold = jnp.array(0.0, jnp.float32)
        temperature = jnp.array(1.0, jnp.float32)
        return {'x': x, 'Wq': Wq, 'bq': bq, 'Wk': Wk, 'bk': bk, 'Wv': Wv, 'bv': bv, 'Wo': Wo, 'bo': bo, 'phase': phase, 'threshold': threshold, 'temperature': temperature}
    _L0_attn_in = _L0_attn_setup()

    def _L0_ffn_setup():
        import jax, jax.numpy as jnp
        import numpy as np
        NUM_EXPERTS = 8
        TOP_K = 2
        DIM = 128
        HIDDEN = 512
        B, S = (4, 256)
        key = jax.random.key(seed)
        ks = jax.random.split(key, 6)
        scale = 0.02
        x = jax.random.normal(ks[0], (B, S, DIM), dtype=jnp.float32)
        wg = jax.random.normal(ks[1], (NUM_EXPERTS, DIM), dtype=jnp.float32) * scale
        bg = jnp.zeros((NUM_EXPERTS,), dtype=jnp.float32)
        Wgate = jax.random.normal(ks[2], (NUM_EXPERTS, HIDDEN, DIM), dtype=jnp.float32) * scale
        Wup = jax.random.normal(ks[3], (NUM_EXPERTS, HIDDEN, DIM), dtype=jnp.float32) * scale
        Wdown = jax.random.normal(ks[4], (NUM_EXPERTS, DIM, HIDDEN), dtype=jnp.float32) * scale
        return {'x': x, 'wg': wg, 'bg': bg, 'Wgate': Wgate, 'Wup': Wup, 'Wdown': Wdown}
    _L0_ffn_in = _L0_ffn_setup()
    _d = {'L0_attn_x': _L0_attn_in['x'], 'L0_attn_Wq': _L0_attn_in['Wq'], 'L0_attn_bq': _L0_attn_in['bq'], 'L0_attn_Wk': _L0_attn_in['Wk'], 'L0_attn_bk': _L0_attn_in['bk'], 'L0_attn_Wv': _L0_attn_in['Wv'], 'L0_attn_bv': _L0_attn_in['bv'], 'L0_attn_Wo': _L0_attn_in['Wo'], 'L0_attn_bo': _L0_attn_in['bo'], 'L0_attn_phase': _L0_attn_in['phase'], 'L0_attn_threshold': _L0_attn_in['threshold'], 'L0_attn_temperature': _L0_attn_in['temperature'], 'L0_ffn_wg': _L0_ffn_in['wg'], 'L0_ffn_bg': _L0_ffn_in['bg'], 'L0_ffn_Wgate': _L0_ffn_in['Wgate'], 'L0_ffn_Wup': _L0_ffn_in['Wup'], 'L0_ffn_Wdown': _L0_ffn_in['Wdown']}
    _x0 = _d['L0_attn_x']
    _d['L0_attn_x'] = jax.random.normal(jax.random.fold_in(jax.random.key(seed), 1), (8, 512, 128), dtype=_x0.dtype)
    del _x0
    return _d

def reference(L0_attn_x, L0_attn_Wq, L0_attn_bq, L0_attn_Wk, L0_attn_bk, L0_attn_Wv, L0_attn_bv, L0_attn_Wo, L0_attn_bo, L0_attn_phase, L0_attn_threshold, L0_attn_temperature, L0_ffn_wg, L0_ffn_bg, L0_ffn_Wgate, L0_ffn_Wup, L0_ffn_Wdown):

    def _L0_attn_ref(x, Wq, bq, Wk, bk, Wv, bv, Wo, bo, phase, threshold, temperature):
        import jax, jax.numpy as jnp
        import numpy as np
        import math
        NUM_HEADS = 16
        TPMS_WEIGHT = 0.3
        TWO_PI = 2.0 * math.pi

        def _tpms_mask(L, phase, threshold, temperature):
            pos = jnp.arange(L, dtype=jnp.float32) / L * TWO_PI
            pq = pos[None, :, None] + phase[:, 0][:, None, None]
            pk = pos[None, None, :] + phase[:, 1][:, None, None]
            pz = (pos[None, :, None] + pos[None, None, :]) * 0.5 + phase[:, 2][:, None, None]
            t = jax.lax.stop_gradient(threshold)
            val = jnp.sin(pq) * jnp.cos(pk) + jnp.sin(pk) * jnp.cos(pz) + jnp.sin(pz) * jnp.cos(pq) - t
            return jax.nn.sigmoid(val / (temperature + 1e-06))
        B, L, H = x.shape
        nh = NUM_HEADS
        hd = H // nh
        scale = math.sqrt(hd)
        Q = (x @ Wq + bq).reshape(B, L, nh, hd).transpose(0, 2, 1, 3)
        K = (x @ Wk + bk).reshape(B, L, nh, hd).transpose(0, 2, 1, 3)
        V = (x @ Wv + bv).reshape(B, L, nh, hd).transpose(0, 2, 1, 3)
        scores = jnp.einsum('bhqd,bhkd->bhqk', Q, K) / scale
        mask = _tpms_mask(L, phase, threshold, temperature)
        scores = scores + TPMS_WEIGHT * jnp.log(mask + 1e-06)[None]
        attn = jax.nn.softmax(scores, axis=-1)
        out = jnp.einsum('bhqk,bhkd->bhqd', attn, V)
        out = out.transpose(0, 2, 1, 3).reshape(B, L, H)
        return out @ Wo + bo

    def _L0_ffn_ref(x, wg, bg, Wgate, Wup, Wdown):
        import jax, jax.numpy as jnp
        import numpy as np
        NUM_EXPERTS = 8
        TOP_K = 2
        DIM = 128
        HIDDEN = 512
        B, S = (4, 256)
        b, s, d = x.shape
        xf = x.reshape(-1, d)
        T = xf.shape[0]
        logits = xf @ wg.T + bg
        vals, idx = jax.lax.top_k(logits, TOP_K)
        masked = jnp.full_like(logits, -jnp.inf)
        rows = jnp.arange(T)[:, None]
        masked = masked.at[rows, idx].set(vals)
        weights = jax.nn.softmax(masked, axis=-1)
        out = jnp.zeros_like(xf)
        for e in range(NUM_EXPERTS):
            g = xf @ Wgate[e].T
            u = xf @ Wup[e].T
            h = g * jax.nn.sigmoid(g) * u
            out = out + h @ Wdown[e].T * weights[:, e:e + 1]
        return out.reshape(b, s, d)
    x = L0_attn_x
    x = _layernorm(x + _L0_attn_ref(x, L0_attn_Wq, L0_attn_bq, L0_attn_Wk, L0_attn_bk, L0_attn_Wv, L0_attn_bv, L0_attn_Wo, L0_attn_bo, L0_attn_phase, L0_attn_threshold, L0_attn_temperature), axis=-1)
    x = _layernorm(x + _L0_ffn_ref(x, L0_ffn_wg, L0_ffn_bg, L0_ffn_Wgate, L0_ffn_Wup, L0_ffn_Wdown), axis=-1)
    return x

_drawn_inputs = setup_inputs


def setup_inputs(seed=0):
    import zlib

    import numpy as np

    out = dict(_drawn_inputs(seed))
    spreads = {'L0_attn_bq': (0.0, 0.8),
     'L0_attn_bk': (0.0, 0.8),
     'L0_attn_bv': (0.0, 0.379),
     'L0_attn_bo': (0.0, 0.1),
     'L0_ffn_bg': (0.0, 0.8)}
    factors = {'L0_attn_Wq': 8.0,
     'L0_attn_Wk': 8.0,
     'L0_attn_Wv': 8.0,
     'L0_attn_Wo': 2.942,
     'L0_attn_phase': 8.0,
     'L0_ffn_wg': 8.0,
     'L0_ffn_Wgate': 6.833,
     'L0_ffn_Wup': 6.81,
     'L0_ffn_Wdown': 6.808}
    for name, (base, spread) in spreads.items():
        noise = np.random.default_rng([zlib.crc32(name.encode()), seed]).standard_normal(out[name].shape)
        drawn = base * np.exp(spread * noise) if base else spread * noise
        out[name] = jnp.asarray(drawn.astype(out[name].dtype))
    for name, factor in factors.items():
        out[name] = (out[name] * factor).astype(out[name].dtype)
    return out
```

```python
import math
from contextlib import ExitStack

import numpy as np

import concourse.bass as bass
from concourse import mybir

F32 = mybir.dt.float32
BF16 = mybir.dt.bfloat16
I32 = mybir.dt.int32
U32 = mybir.dt.uint32
ALU = mybir.AluOpType
ACT = mybir.ActivationFunctionType
AX = mybir.AxisListType

P = 128
B, L, H = 8, 512, 128
T = B * L
NH, HD = 16, 8
NE, HID = 8, 512
NT = T // P
QB = 4
NU = NH * (B // QB)
KC = L // P
UC = QB * L
ROWS = 6 * HD
MROW = 64
NF = 5
RING = 4
ET = 2 * T // P + NE
FILLS = 8
XW = H + 2
EPS = 1e-5
TPMS = 0.3
TWO_PI = 2.0 * math.pi
C1 = 6.28125
C2 = TWO_PI - C1
MAGIC = 1.5 * 2.0 ** 23
POOL_B = 3


def wait(eng, sem, value):
    if isinstance(value, int) and value <= 0:
        return
    eng.wait_ge(sem, value)


def wait_alone(eng, turn, sem, value):
    wait(eng, sem, value)
    if not isinstance(value, int):
        eng.sem_inc(turn, 1)


def build(nc, a, out):
    ctx = ExitStack()
    with ctx:
        def sb(name, shape, dt=F32):
            return ctx.enter_context(nc.sbuf_tensor(name, shape, dt))

        def sem(name):
            return ctx.enter_context(nc.semaphore(name))

        def dram(name, shape, dt=F32):
            return nc.dram_tensor(name, shape, dt, kind="Internal").ap()

        q_dram = dram("q_parts", (6, P, T), BF16)
        k_dram = dram("k_parts", (6, P, T), BF16)
        f_dram = dram("mask_key_factors", (P, NF, 64))
        g_dram = dram("mask_query_factors", (P, NF, 64))
        o_dram = dram("head_outputs", (NH, HD + 1, T))
        xs_dram = dram("routed_rows", (ET * P, XW))
        y_dram = dram("expert_rows", (2 * T + ET * P, H))

        arena = sb("arena", [P, 16384])
        probs = [arena[:, 2048 * i:2048 * (i + 1)] for i in range(KC)]
        qs = [arena[:, 8192 + 1024 * i:8192 + 1024 * (i + 1)].bitcast(BF16) for i in range(RING)]
        ks = [arena[:, 12288 + 1024 * i:12288 + 1024 * (i + 1)].bitcast(BF16) for i in range(RING)]
        xb = [arena[:, 512 * i:512 * (i + 1)] for i in range(2)]
        qkf = [arena[:, 1024 + 1024 * i:2048 + 1024 * i].rearrange("p (s t) -> p s t", s=2) for i in range(2)]
        qkr = [arena[:, 3072 + 1024 * i:4096 + 1024 * i].rearrange("p (s t) -> p s t", s=2) for i in range(2)]
        parts = [arena[:, 5120 + 1536 * i:6656 + 1536 * i].bitcast(BF16).rearrange(
            "p (n s t) -> p n s t", n=3, s=2) for i in range(2)]
        XA = NT * XW
        xa = [arena[:, XA * s:XA * (s + 1)].rearrange("p (t c) -> p t c", c=XW) for s in range(2)]
        resid = arena[:, 2 * XA:2 * XA + NT * H].rearrange("p (t c) -> p t c", c=H)
        z_all = arena[:, XA:XA + NT * H].rearrange("p (t c) -> p t c", c=H)
        yg = [[arena[:, 2 * XA + 2048 * i + 1024 * s:2 * XA + 2048 * i + 1024 * (s + 1)].rearrange(
            "p (t c) -> p t c", c=H) for s in range(2)] for i in range(2)]
        R2 = 2 * XA + NT * H
        oT = [arena[:, R2 + 512 * i:R2 + 512 * (i + 1)] for i in range(2)]
        aT = [arena[:, R2 + 1024 + 512 * i:R2 + 1024 + 512 * (i + 1)] for i in range(2)]
        x1T = [arena[:, R2 + 2048 + 512 * i:R2 + 2048 + 512 * (i + 1)] for i in range(2)]

        v_all = sb("v_all", [P, NH, NT, HD + 1])
        spare = v_all[:].rearrange("p h t d -> p (h t d)")
        table = lambda k: spare[:, 256 * k:256 * (k + 1)]
        lg, mx, asg, psel = (table(k).rearrange("p (t e) -> p t e", e=NE) for k in range(4))
        oh = [table(4 + k).rearrange("p (t e) -> p t e", e=NE) for k in range(2)]
        inc, exc, posn = (table(6 + k).rearrange("p (e t) -> p e t", e=NE) for k in range(3))
        ix = table(9).bitcast(U32).rearrange("p (t e) -> p t e", e=NE)
        zer = table(10)
        cmp = spare[:, 11 * 256:11 * 256 + ET * NE].rearrange("p (t e) -> p t e", e=NE)
        v_cur = [sb(f"v_cur{i}", [P, NT, HD + 1]) for i in range(2)]
        mask = [sb(f"mask{i}", [P, KC, L]) for i in range(2)]
        sg = [mask[0][:, i, :] for i in range(2)]
        sel = mask[0][:, 0:2, :].rearrange("p k (b c) -> p (k b) c", c=P)
        hh = [mask[0][:, 2 + i, :] for i in range(2)]
        stats = mask[1][:, 2, 0:NT * 6].rearrange("p (t c) -> p t c", c=6)
        mv = mask[1][:, 2, NT * 6:NT * 8].rearrange("p (t c) -> p t c", c=2)
        hT = [mask[1][:, i, :] for i in range(2)]
        e_buf = [sb(f"e_buf{i}", [P, 2, L]) for i in range(2)]
        l_buf = sb("l_buf", [P, 2, L])
        den, rden = e_buf[0][:, 0, :], e_buf[0][:, 1, :]
        l_flat = l_buf[:].rearrange("p i t -> p (i t)")
        xs = [l_flat[:, XW * i:XW * (i + 1)] for i in range(4)]
        xT = [e_buf[1][:, 0, P * i:P * (i + 1)] for i in range(2)]
        yo = [e_buf[1][:, 1, P * i:P * (i + 1)] for i in range(4)]
        fac = [sb(f"fac{i}", [NF, 2, 8, 64]) for i in range(2)]
        o_sb = [sb(f"o_sb{i}", [P, L]) for i in range(2)]
        xbo = sb("xbo", [P, NT, H])
        wgate = sb("wgate", [P, NE * HID])
        wup = sb("wup", [P, NE * HID])
        wdown = sb("wdown", [P, NE * HID])
        wqkvo = sb("wqkvo", [P, 4, H])
        bqk = sb("bqk", [P, 2])
        bqs = sb("bqs", [P, 1])
        bvb = sb("bvb", [P, H])
        bob = sb("bob", [P, H])
        wr = sb("wr", [P, NE])
        bgb = sb("bgb", [P, NE])
        ph = sb("ph", [P, 3])
        tt = sb("tt", [P, 2])
        tmp1 = sb("tmp1", [P, 4])
        pos = sb("pos", [P, 5, 64])
        ang = sb("ang", [P, 3, 64])
        rnd = sb("rnd", [P, 3, 64])
        aby = sb("aby", [P, 3, 64])
        sn = sb("sn", [P, 3, 64])
        cs = sb("cs", [P, 3, 64])
        fk = sb("fk", [P, NF, 64])
        gq = sb("gq", [P, NF, 64])
        bias = sb("bias", [P, 5])
        bias2 = sb("bias2", [P, 1])
        ident = sb("ident", [P, P])
        neg_max = sb("neg_max", [P, RING, 16])
        m_parts = sb("m_parts", [16, RING, 2, P], BF16)
        sd = sb("sd", [P, NT])
        rstd = sb("rstd", [P, NT])
        ixf = sb("ixf", [P, NT, 2])
        iota8 = sb("iota8", [P, NE])
        iotat = sb("iotat", [P, ET])
        destc = sb("destc", [P, 2, NT], I32)
        tri = sb("tri", [P, P])
        ones = sb("ones", [P, P])
        cnt = sb("cnt", [P, NE])
        cnti = sb("cnti", [P, NE], I32)
        tls = sb("tls", [P, NE])
        cumt = sb("cumt", [P, NE])
        base = sb("base", [P, NE])
        slotf = sb("slotf", [P, 2, NT])
        slot = sb("slot", [P, 2, NT], I32)
        tef = sb("tef", [P, ET])
        te = sb("te", [P, ET], I32)
        dlt = sb("dlt", [P, NT])
        edl = sb("edl", [P, NT])
        edp = sb("edp", [P, NT])

        banks = [ctx.enter_context(nc.psum_tensor(f"bank{i}", [P, 1024], F32)) for i in range(4)]
        st = [banks[0], banks[1]]
        sm = [banks[2][:, 0:512], banks[2][:, 512:1024]]
        pv = banks[3][:, 0:512]
        misc = banks[3][:, 512:1024]

        names = """consts_loaded weights_loaded expert_w_loaded trig_ready sincos_ready
        factors_ready proj_ready v_ready evac_done v_used split_step split_done xbo_ready
        st_ready exp_done sm_ready sm_done max_ready mt_ready mt_used msub
        val_ready val_used clamp_done ln_done sub_done mask_ready
        v_cur_ready pv_step pv_evac pool_mul dve_mul pv_init sp_turn pool_turn sel_loaded
        den_loaded rden_ready bc_ready aT_ready y_ready resid_ready stats_done mv_done sd_ready
        x1_ready x1b_ready x1t_ready x1t_copied logit_ready edelta_ready rw_ready count_ready slots_ready
        tiles_ready filled scattered dlink zeroed
        xT_ready xT_copied gu_ready silu_done h_ready hT_ready hT_copied yt_ready yo_ready y_scattered
        z_ready z_stats sd2_ready out_ready stored dest_ready f_stored cast""".split()
        S = {n: sem(n) for n in names}
        s2 = {n: [sem(f"{n}{i}") for i in range(k)] for n, k in
              (("x_loaded", 2), ("parts_stored", 2), ("qk_loaded", 4), ("m_loaded", 4), ("fac_loaded", 2),
               ("o_stored", 2), ("oT_loaded", 2), ("xs_loaded", 4), ("yg_loaded", 2))}

        block = ctx.enter_context(nc.Block())

        def loop(eng, first, last, body, peel_last):
            body(first)
            with eng.Fori(first + 1, last - (1 if peel_last else 0)) as g:
                body(g)
            if peel_last:
                body(last - 1)

        CONST = [(ident, "c_ident"), (pos, "c_pos"), (iota8, "c_iota8"),
                 (iotat, "c_iotat"), (destc, "c_dest"), (tri, "c_tri"), (ph, "phase"), (bqk, "bqk")]

        @block.sync
        def _(sp):
            for t, n in CONST:
                sp.dma_start(t[:], a[n]).then_inc(S["consts_loaded"], 16)
            for t, n in ((bvb, "bv"), (bob, "bo"), (bgb, "bg"), (tt[:, 0:1], "thr"), (tt[:, 1:2], "temp")):
                t = t if n in ("thr", "temp") else t[:]
                sp.dma_start(t, a[n].partition_broadcast(P)).then_inc(S["consts_loaded"], 16)
            sp.dma_start(wr[:], a["wg"]).then_inc(S["consts_loaded"], 16)
            for i, n in enumerate(("Wq", "Wk", "Wv", "Wo")):
                sp.dma_start(wqkvo[:, i, :], a[n]).then_inc(S["weights_loaded"], 16)
            sp.dma_start(xbo[:], a["x_tok"].rearrange("(t p) c -> p t c", p=P)).then_inc(S["consts_loaded"], 16)

            def load_x(g, i):
                wait_alone(sp, S["sp_turn"], S["v_ready"], 2 * g + i - 1)
                sp.dma_start(xb[i], a["xT"][:, bass.ds((2 * g + i) * L, L)]).then_inc(s2["x_loaded"][i], 16)

            def project(g):
                for i in range(2):
                    load_x(g, i)
                for i in range(2):
                    wait_alone(sp, S["sp_turn"], S["split_done"], 2 * g + i + 1)
                    for side, dr, order in ((0, q_dram, (0, 0, 0, 1, 1, 2)), (1, k_dram, (0, 1, 2, 0, 1, 0))):
                        for j, n in enumerate(order):
                            sp.dma_start(dr[j, :, bass.ds((2 * g + i) * L, L)],
                                         parts[i][:, n, side, :]).then_inc(s2["parts_stored"][i], 16)

            loop(sp, 0, 4, project, False)
            sp.wait_ge(S["factors_ready"], 1)
            sp.dma_start(f_dram, fk[:]).then_inc(S["f_stored"], 16)
            sp.dma_start(g_dram, gq[:]).then_inc(S["f_stored"], 16)
            for i in range(2):
                sp.wait_ge(s2["parts_stored"][i], 16 * 12 * 4)
            sp.wait_ge(S["f_stored"], 32)

            def load_fac(slot_, hv):
                for s, dr in ((0, f_dram), (1, g_dram)):
                    sp.dma_start(fac[slot_][:, s], dr[bass.ds(hv * 8, 8)].rearrange("c f t -> f c t")
                                 ).then_inc(s2["fac_loaded"][slot_], 16)

            def load_qk(r, head, q):
                sp.dma_start(qs[r][0:ROWS, :], q_dram[:, bass.ds(head * HD, HD), q * UC:(q + 1) * UC]
                             ).then_inc(s2["qk_loaded"][r], 16)
                sp.dma_start(ks[r][0:ROWS, :], k_dram[:, bass.ds(head * HD, HD), q * UC:(q + 1) * UC]
                             ).then_inc(s2["qk_loaded"][r], 16)
                sp.dma_start(qs[r][MROW:MROW + 2, :], ks[r][MROW + 2:MROW + 4, :]).then_inc(s2["qk_loaded"][r], 16)

            def store_max(r):
                for n in range(2):
                    sp.dma_start(qs[r][MROW + n:MROW + n + 1, :], m_parts[:, r, n, :]
                                 ).then_inc(s2["m_loaded"][r], 16)

            def store_o(par, head, q):
                for b in range(QB):
                    c = (q * QB + b) * L
                    sp.dma_start(o_dram[bass.ds(head, 1), :, c:c + L], o_sb[par][32 * b:32 * b + HD + 1, :]
                                 ).then_inc(s2["o_stored"][par], 16)

            sp.wait_ge(S["zeroed"], 2)
            load_fac(0, 0)
            load_fac(1, 1)
            for u in range(RING):
                load_qk(u, u // 2, u % 2)
            for t, n in ((wgate, "Wgate"), (wup, "Wup"), (wdown, "Wdown")):
                sp.dma_start(t[:], a[n]).then_inc(S["expert_w_loaded"], 16)
            for i in range(FILLS):
                n = ET * P // FILLS
                sp.dma_start(xs_dram[i * n:(i + 1) * n, :], a["c_fill"][i * n:(i + 1) * n, :]
                             ).then_inc(S["filled"], 16)
            sp.wait_ge(S["mt_used"], 1)
            store_max(0)

            def attend(g):
                peeled = isinstance(g, int)
                for r in range(4):
                    u = 4 * g + r
                    lastg = peeled and g == NU // 4 - 1
                    if not (lastg and r == 3):
                        wait_alone(sp, S["sp_turn"], S["mt_used"], u + 2)
                        store_max((r + 1) % 4)
                    if not (peeled and u == 0):
                        wait_alone(sp, S["sp_turn"], S["pv_evac"], u)
                        store_o((r + 1) % 2, 2 * g + (r - 1) // 2, (r + 1) % 2)
                    hf = 2 * g + r // 2 + 2
                    if r % 2 == 0 and not (peeled and g == NU // 4 - 1):
                        wait_alone(sp, S["sp_turn"], S["val_ready"], 4 * hf - 4)
                        load_fac((r // 2) % 2, hf)
                    if not lastg:
                        wait_alone(sp, S["sp_turn"], S["st_ready"], 8 * (u + 1))
                        load_qk(r, 2 * (g + 1) + r // 2, r % 2)

            loop(sp, 0, NU // 4, attend, True)
            sp.wait_ge(S["pv_evac"], NU)
            store_o((NU - 1) % 2, NH - 1, 1)
            for i in range(2):
                sp.wait_ge(s2["o_stored"][i], 64 * NU // 2)
            sp.wait_ge(S["pool_mul"], NU * KC)
            sp.wait_ge(S["dve_mul"], NU * KC)
            sp.dma_start(sel, a["c_sel"]).then_inc(S["sel_loaded"], 16)
            sp.dma_start(den, o_dram[:, HD, :].rearrange("h (b t) -> h b t", b=B)).then_inc(S["den_loaded"], 16)

            def load_oT(g):
                for i in range(2):
                    wait_alone(sp, S["sp_turn"], S["aT_ready"], 2 * g + i - 1)
                    sp.dma_start(oT[i], o_dram[:, 0:HD, bass.ds((2 * g + i) * L, L)]
                                 ).then_inc(s2["oT_loaded"][i], 16)

            loop(sp, 0, 4, load_oT, False)
            sp.wait_ge(S["scattered"], 16 * 2 * NT)

            def load_xs(g):
                for r in range(4):
                    i = 4 * g + r
                    wait_alone(sp, S["sp_turn"], S["y_scattered"], 16 * (i - 3))
                    sp.dma_start(xs[r], xs_dram[bass.ds(i * P, P), :]).then_inc(s2["xs_loaded"][r], 16)

            loop(sp, 0, ET // 4, load_xs, False)
            sp.wait_ge(S["y_scattered"], 16 * ET)
            for k in range(4):
                if k >= 2:
                    wait_alone(sp, S["sp_turn"], S["z_ready"], k - 1)
                for s in range(2):
                    sp.dma_start(yg[k % 2][s], y_dram[s * T + k * 1024:s * T + (k + 1) * 1024, :].rearrange(
                        "(t p) c -> p t c", p=P)).then_inc(s2["yg_loaded"][k % 2], 16)
            for k in range(4):
                wait_alone(sp, S["sp_turn"], S["out_ready"], k + 1)
                sp.dma_start(out[k * 1024:(k + 1) * 1024, :].rearrange("(t p) c -> p t c", p=P),
                             z_all[:, 8 * k:8 * k + 8, :]).then_inc(S["stored"], 16)
            sp.wait_ge(S["stored"], 64)

        @block.tensor
        def _(pe):
            mm = nc.tensor.matmul
            pe.wait_ge(S["weights_loaded"], 64)

            def project(g):
                for i in range(2):
                    b = 2 * g + i
                    pe.wait_ge(s2["x_loaded"][i], 16 * (g + 1))
                    wait(pe, S["evac_done"], b - 1)
                    for s in range(2):
                        last = mm(st[i][:, s * L:(s + 1) * L], wqkvo[:, s, :], xb[i], start=True, stop=True)
                    last.then_inc(S["proj_ready"], 1)
                    wait(pe, S["v_used"], b - 1)
                    for c in range(4):
                        last = mm(sm[i][:, c * P:(c + 1) * P], xb[i][:, c * P:(c + 1) * P], wqkvo[:, 2, :],
                                  start=True, stop=True)
                    last.then_inc(S["v_ready"], 1)

            loop(pe, 0, 4, project, False)

            def s_chunk(r, b, c, k):
                pe.wait_ge(S["sm_done"], k - 1) if not (isinstance(k, int) and k < 2) else None
                mm(sm[c % 2], qs[r][:, b * L + c * P:b * L + (c + 1) * P], ks[r][:, b * L:(b + 1) * L],
                   start=True, stop=True).then_inc(S["sm_ready"], 1)

            def turn_max(r, u):
                pe.wait_ge(S["max_ready"], u + 1)
                nc.tensor.transpose(misc[0:16, 0:P], neg_max[:, r, :], ident[:]).then_inc(S["mt_ready"], 1)

            def mask_arg(par, kc):
                mm(misc, fac[par][:, 0].rearrange("f c t -> f (c t)")[:, kc * P:(kc + 1) * P],
                   fac[par][:, 1].rearrange("f c t -> f (c t)"), start=True, stop=True
                   ).then_inc(S["val_ready"], 1)

            pe.wait_ge(S["evac_done"], B)
            pe.wait_ge(S["v_used"], B)
            for v in range(6):
                if v % 4 == 0:
                    pe.wait_ge(s2["fac_loaded"][v // 4], 32)
                wait(pe, S["val_used"], v)
                mask_arg(v // 4, v % 4)
            for u in range(2):
                pe.wait_ge(s2["qk_loaded"][u], 48)
                for k in range(16):
                    s_chunk(u, k // 4, k % 4, 16 * u + k)
            pe.wait_ge(S["val_used"], 6)
            turn_max(0, 0)
            pe.wait_ge(S["pv_init"], 1)

            def sums(par, kc, n, u):
                pe.wait_ge(S["pool_mul"], n + 1)
                pe.wait_ge(S["dve_mul"], n + 1)
                if kc == 0:
                    wait(pe, S["pv_evac"], u)
                hpar, q = par
                for b in range(QB):
                    last = mm(pv[32 * b:32 * b + HD + 1, :], v_cur[hpar][:, (q * QB + b) * KC + kc, :],
                              probs[kc][:, b * L:(b + 1) * L], start=(kc == 0), stop=(kc == KC - 1))
                last.then_inc(S["pv_step"], 1)

            def attend(g):
                peeled = isinstance(g, int)
                for r in range(4):
                    u = 4 * g + r
                    last_s = peeled and u >= NU - 2
                    r2 = (r + 2) % 4
                    for kc in range(KC):
                        n = 4 * u + kc
                        if kc == 0:
                            pe.wait_ge(s2["m_loaded"][r], 32 * (g + 1))
                            if not last_s:
                                pe.wait_ge(s2["qk_loaded"][r2], 48 * (g + (1 if r < 2 else 2)))
                        for half in range(2):
                            wait(pe, S["exp_done"], 2 * n + half - 1)
                            for i in range(2):
                                b = 2 * half + i
                                last = mm(st[half][:, i * L:(i + 1) * L],
                                          ks[r][:, b * L + kc * P:b * L + (kc + 1) * P],
                                          qs[r][:, b * L:(b + 1) * L], start=True, stop=True)
                            last.then_inc(S["st_ready"], 1)
                            if not last_s:
                                s_chunk(r2, kc, half, 16 * (u + 2) + 4 * kc + half)
                        if kc == 0 and not (peeled and u == NU - 1):
                            wait(pe, S["val_used"], 6 + 2 * u) if not (peeled and u > NU - 4) else None
                            turn_max((r + 1) % 4, u + 1)
                        if kc in (1, 2) and not (peeled and u + 3 >= NU):
                            if kc == 1:
                                pe.wait_ge(S["mt_used"], u + 2)
                                hv = (r + 3) // 2
                                pe.wait_ge(s2["fac_loaded"][hv % 2], 32 * (g + 1 + hv // 2))
                            else:
                                pe.wait_ge(S["val_used"], 6 + 2 * u + 1)
                            mask_arg(((r + 3) // 2) % 2, 2 * ((r + 3) % 2) + kc - 1)
                        if not last_s:
                            s_chunk(r2, kc, 2, 16 * (u + 2) + 4 * kc + 2)
                        if not (peeled and n < 2):
                            pn = (kc + 2) % 4
                            pr = r if kc >= 2 else r - 1
                            if pn == 0 and pr % 2 == 0:
                                pe.wait_ge(S["v_cur_ready"], 2 * g + (pr // 2) + 1)
                            sums((((pr // 2) % 2), pr % 2), pn, n - 2, 4 * g + pr)
                        if not last_s:
                            s_chunk(r2, kc, 3, 16 * (u + 2) + 4 * kc + 3)

            loop(pe, 0, NU // 4, attend, True)
            for n in (NU * KC - 2, NU * KC - 1):
                sums((1, 1), n % 4, n, NU - 1)

            pe.wait_ge(S["consts_loaded"], 16 * (len(CONST) + 7))
            pe.wait_ge(S["rden_ready"], 1)
            pe.wait_ge(S["sel_loaded"], 16)
            for b in range(B):
                i = b % 2
                wait(pe, S["aT_ready"], b - 1)
                mm(st[i][:, 0:L], sel[:, b, :], rden, start=True, stop=True).then_inc(S["bc_ready"], 1)
                pe.wait_ge(S["aT_ready"], b + 1)
                wait(pe, S["resid_ready"], b - 1)
                for c in range(4):
                    last = mm(st[i][:, L + c * P:L + (c + 1) * P], aT[i][:, c * P:(c + 1) * P], wqkvo[:, 3, :],
                              start=True, stop=True)
                last.then_inc(S["y_ready"], 1)
            for b in range(B):
                i = b % 2
                pe.wait_ge(S["x1_ready"], 4 * (b + 1))
                wait(pe, S["x1t_copied"], b - 1)
                for c in range(4):
                    last = nc.tensor.transpose(sm[i][:, c * P:(c + 1) * P], xa[0][:, 4 * b + c, 0:H], ident[:])
                last.then_inc(S["x1t_ready"], 1)
                pe.wait_ge(S["x1t_copied"], b + 1)
                for c in range(4):
                    t = 4 * b + c
                    last = mm(pv[:, t * NE:(t + 1) * NE], x1T[i][:, c * P:(c + 1) * P], wr[:],
                              start=True, stop=True)
            last.then_inc(S["logit_ready"], 1)
            pe.wait_ge(S["count_ready"], 1)
            av = asg.rearrange("p t e -> p e t")
            mm(misc[:, 0:256], tri[:], av, start=True, stop=True)
            mm(misc[:, 256:512], ones[:], av, start=True, stop=True).then_inc(S["slots_ready"], 1)

            gb = [banks[0][:, 0:512], banks[1][:, 0:512]]
            ub = [banks[0][:, 512:1024], banks[1][:, 512:1024]]
            xtp, htp = banks[2][:, 0:512], banks[2][:, 512:1024]
            yp = banks[3]
            pe.wait_ge(S["tiles_ready"], 1)
            pe.wait_ge(S["expert_w_loaded"], 48)

            def turn_x(r, i, g):
                pe.wait_ge(s2["xs_loaded"][r], 16 * (g + 1))
                wait(pe, S["xT_copied"], i)
                nc.tensor.transpose(xtp[:, 0:P], xs[r][:, 0:H], ident[:]).then_inc(S["xT_ready"], 1)

            def expert_of(i):
                return pe.value_load(te[0:1, bass.ds(i, 1)], min_val=0, max_val=NE - 1)

            def down(r, i):
                e = expert_of(i)
                pe.wait_ge(S["hT_copied"], i + 1)
                wait(pe, S["yo_ready"], i - 1)
                for c in range(4):
                    last = mm(yp[:, 512 * (r % 2):512 * (r % 2) + H], hT[r % 2][:, c * P:(c + 1) * P],
                              wdown[:, bass.ds(e * HID + c * P, P)], start=(c == 0), stop=(c == 3))
                last.then_inc(S["yt_ready"], 1)

            def turn_h(r, i):
                pe.wait_ge(S["h_ready"], i + 1)
                wait(pe, S["hT_copied"], i)
                for c in range(4):
                    last = nc.tensor.transpose(htp[:, c * P:(c + 1) * P], hh[r % 2][:, c * P:(c + 1) * P], ident[:])
                last.then_inc(S["hT_ready"], 1)

            turn_x(0, 0, 0)

            def expert(g):
                peeled = isinstance(g, int)
                for r in range(4):
                    i = 4 * g + r
                    e = expert_of(i)
                    pe.wait_ge(S["xT_copied"], i + 1)
                    wait(pe, S["h_ready"], i - 1)
                    mm(gb[r % 2], xT[r % 2], wgate[:, bass.ds(e * HID, HID)], start=True, stop=True)
                    mm(ub[r % 2], xT[r % 2], wup[:, bass.ds(e * HID, HID)], start=True, stop=True
                       ).then_inc(S["gu_ready"], 1)
                    if not (peeled and i + 1 >= ET):
                        turn_x((r + 1) % 4, i + 1, g + (1 if r == 3 else 0))
                    if not (peeled and i < 2):
                        down((r + 2) % 4, i - 2)
                    if not (peeled and i < 1):
                        turn_h((r + 3) % 4, i - 1)

            loop(pe, 0, ET // 4, expert, True)
            down(2, ET - 2)
            turn_h(3, ET - 1)
            down(3, ET - 1)

        @block.scalar
        def _(act):
            A = nc.scalar.activation
            RS = 1.0 / math.sqrt(HD)
            act.wait_ge(S["trig_ready"], 1)
            A(sn[:], ang[:], ACT.Sin)
            A(cs[:], aby[:], ACT.Sin, bias=bias[:, 0:1], scale=-1.0).then_inc(S["sincos_ready"], 1)
            nc.scalar.preload_act_table_set("natural_log_exp_and_others")

            def project(g):
                for i in range(2):
                    b = 2 * g + i
                    act.wait_ge(S["proj_ready"], b + 1)
                    wait(act, s2["parts_stored"][i], 16 * 12 * g)
                    A(qkf[i][:, 0, :], st[i][:, 0:L], ACT.Identity, bias=bqs[:], scale=RS)
                    A(parts[i][:, 0, 0, :], st[i][:, 0:L], ACT.Identity, bias=bqs[:], scale=RS)
                    A(qkf[i][:, 1, :], st[i][:, L:2 * L], ACT.Identity, bias=bqk[:, 1:2])
                    A(parts[i][:, 0, 1, :], st[i][:, L:2 * L], ACT.Identity, bias=bqk[:, 1:2]
                      ).then_inc(S["evac_done"], 1)

            act.wait_ge(S["consts_loaded"], 16 * (len(CONST) + 7))
            loop(act, 0, 4, project, False)

            def mask_exp(v, par, i):
                act.wait_ge(S["val_ready"], v + 1)
                A(e_buf[par][:, i, :], misc, ACT.Exp, bias=bias[:, 3:4], scale=bias[:, 2:3]
                  ).then_inc(S["val_used"], 1)

            def mask_ln(w, par):
                act.wait_ge(S["clamp_done"], w + 1)
                wait(act, S["mask_ready"], w)
                A(l_buf[:], e_buf[par][:], ACT.Ln, bias=bias[:, 4:5], scale=1e-6)
                A(e_buf[par][:], e_buf[par][:], ACT.Ln, bias=bias[:, 1:2]).then_inc(S["ln_done"], 1)

            def mask_fin(w, hpar, pair):
                act.wait_ge(S["sub_done"], w + 1)
                A(mask[hpar][:, 2 * pair:2 * pair + 2, :], l_buf[:], ACT.Exp, scale=TPMS).then_inc(S["mask_ready"], 1)

            def take_v(head, par):
                nc.scalar.copy(v_cur[par][:], v_all[:, head]).then_inc(S["v_cur_ready"], 1)

            act.wait_ge(S["cast"], 1)
            for w in range(3):
                if w == 2:
                    act.wait_ge(S["sub_done"], 1)
                for i in range(2):
                    mask_exp(2 * w + i, w % 2, i)
                if w < 2:
                    mask_ln(w, w % 2)
                    mask_fin(w, 0, w)
            act.wait_ge(S["v_used"], B)
            nc.scalar.copy(v_cur[0][:], v_all[:, 0]).then_inc(S["v_cur_ready"], 1)
            act.wait_ge(S["split_done"], B)
            for i in range(2):
                act.wait_ge(s2["parts_stored"][i], 16 * 12 * 4)

            def attend(g):
                peeled = isinstance(g, int)
                for r in range(4):
                    u = 4 * g + r
                    for kc in range(KC):
                        n = 4 * u + kc
                        wait(act, S["pv_step"], n - 3)
                        for half in range(2):
                            act.wait_ge(S["st_ready"], 2 * n + half + 1)
                            A(probs[kc][:, half * 1024:(half + 1) * 1024], st[half][:], ACT.Exp
                              ).then_inc(S["exp_done"], 1)
                        if kc == 0 and not (peeled and u + 2 >= NU):
                            mask_ln(u + 2, r % 2)
                        if kc in (1, 2) and not (peeled and u + 3 >= NU):
                            if kc == 1:
                                act.wait_ge(S["sub_done"], u + 2)
                            mask_exp(6 + 2 * u + kc - 1, (r + 1) % 2, kc - 1)
                        if kc == 2:
                            if not (peeled and u + 2 >= NU):
                                hv = (r + 2) // 2
                                wait(act, S["pool_mul"], 8 * (2 * g + hv - 1))
                                wait(act, S["dve_mul"], 8 * (2 * g + hv - 1))
                                mask_fin(u + 2, hv % 2, r % 2)
                            if not (peeled and u == 0):
                                copy_sums(u - 1, (r + 1) % 2, g, r)
                        if kc == 3 and r % 2 and not (peeled and u == NU - 1):
                            wait(act, S["pv_step"], 8 * (2 * g + r // 2))
                            take_v(2 * g + r // 2 + 1, (r // 2 + 1) % 2)

            def copy_sums(u, par, g, r):
                act.wait_ge(S["pv_step"], 4 * (u + 1))
                wait(act, s2["o_stored"][par], 64 * (2 * g + (0 if r == 0 else (r - 1) // 2)) if r else 64 * (2 * g - 1))
                nc.scalar.copy(o_sb[par][:], pv).then_inc(S["pv_evac"], 1)

            loop(act, 0, NU // 4, attend, True)
            act.wait_ge(S["pv_step"], NU * KC)
            act.wait_ge(s2["o_stored"][1], 64 * (NU // 2 - 1))
            nc.scalar.copy(o_sb[1][:], pv).then_inc(S["pv_evac"], 1)

            act.wait_ge(S["mv_done"], 1)
            A(sd[:], mv[:, :, 1], ACT.Sqrt, bias=bias2[:]).then_inc(S["sd_ready"], 1)
            for b in range(B):
                act.wait_ge(S["x1t_ready"], b + 1)
                nc.scalar.copy(x1T[b % 2], sm[b % 2]).then_inc(S["x1t_copied"], 1)
                nc.scalar.copy(xa[1][:, 4 * b:4 * b + 4, 0:H], xa[0][:, 4 * b:4 * b + 4, 0:H]
                               ).then_inc(S["x1b_ready"], 1)
            act.wait_ge(S["rw_ready"], 1)
            A(edl[:], dlt[:], ACT.Exp).then_inc(S["edelta_ready"], 1)

            gb = [banks[0][:, 0:512], banks[1][:, 0:512]]
            yp = banks[3]

            def x_copy(r, i):
                act.wait_ge(S["xT_ready"], i + 1)
                wait(act, S["gu_ready"], i - 1)
                nc.scalar.copy(xT[r % 2], banks[2][:, 0:P]).then_inc(S["xT_copied"], 1)

            def y_copy(r, i):
                act.wait_ge(S["yt_ready"], i + 1)
                nc.scalar.mul(yo[r], yp[:, 512 * (r % 2):512 * (r % 2) + H], xs[r][:, H + 1:H + 2]
                              ).then_inc(S["yo_ready"], 1)

            x_copy(0, 0)

            def expert(g):
                peeled = isinstance(g, int)
                for r in range(4):
                    i = 4 * g + r
                    act.wait_ge(S["gu_ready"], i + 1)
                    wait(act, S["h_ready"], i - 1)
                    A(sg[r % 2], gb[r % 2], ACT.Silu).then_inc(S["silu_done"], 1)
                    if not (peeled and i + 1 >= ET):
                        x_copy((r + 1) % 4, i + 1)
                    if not (peeled and i < 2):
                        y_copy((r + 2) % 4, i - 2)

            loop(act, 0, ET // 4, expert, True)
            y_copy(2, ET - 2)
            y_copy(3, ET - 1)
            act.wait_ge(S["z_stats"], 1)
            A(sd[:], mv[:, :, 1], ACT.Sqrt, bias=bias2[:]).then_inc(S["sd2_ready"], 1)

        @block.gpsimd
        def _(pool):
            for i in range(RING):
                nc.gpsimd.memset(arena[:, 8192 + 1024 * i:8192 + 1024 * (i + 1)], 0.0)
                last = nc.gpsimd.memset(arena[:, 12288 + 1024 * i:12288 + 1024 * (i + 1)], 0.0)
            last.then_inc(S["zeroed"], 1)
            pool.wait_ge(S["zeroed"], 1)
            for i in range(RING):
                last = nc.gpsimd.memset(ks[i][MROW:MROW + 2, :], 1.0)
            last.then_inc(S["zeroed"], 1)
            pool.wait_ge(S["zeroed"], 2)
            pool.wait_ge(S["consts_loaded"], 16 * (len(CONST) + 7))
            nc.gpsimd.tensor_tensor(xbo[:], xbo[:], bob[:].unsqueeze(1).broadcast_to([P, NT, H]), ALU.add
                                    ).then_inc(S["xbo_ready"], 1)

            def attend(g):
                for r in range(4):
                    for kc in range(KC):
                        n = 4 * (4 * g + r) + kc
                        pool.wait_ge(S["exp_done"], 2 * n + 2)
                        pool.wait_ge(S["mask_ready"], 2 * (2 * g + r // 2) + kc // 2 + 1)
                        pb = probs[kc][:, 0:POOL_B * L].rearrange("p (b t) -> p b t", b=POOL_B)
                        nc.gpsimd.tensor_tensor(
                            pb, pb, mask[r // 2][:, kc, :].unsqueeze(1).broadcast_to([P, POOL_B, L]), ALU.mult
                        ).then_inc(S["pool_mul"], 1)

            loop(pool, 0, NU // 4, attend, False)
            pool.wait_ge(S["filled"], 16 * (FILLS))
            pool.wait_ge(S["dest_ready"], 1)
            pool.wait_ge(S["x1b_ready"], B)
            for s in range(2):
                for t in range(NT):
                    nc.gpsimd.indirect_dma_start(
                        xs_dram, bass.IndirectOffsetOnAxis(ap=slot[:, s, t:t + 1].bitcast(U32), axis=0),
                        xa[s][:, t, :], None).then_inc(S["scattered"], 16)

            def expert(g):
                for r in range(4):
                    i = 4 * g + r
                    wait_alone(pool, S["pool_turn"], S["yo_ready"], i + 1)
                    nc.gpsimd.indirect_dma_start(
                        y_dram, bass.IndirectOffsetOnAxis(ap=xs[r][:, H:H + 1].bitcast(U32), axis=0),
                        yo[r], None).then_inc(S["y_scattered"], 16)

            loop(pool, 0, ET // 4, expert, False)

        @block.vector
        def _(dve):
            V = nc.vector
            chain = [0]

            def link(ins):
                chain[0] += 1
                ins.then_inc(S["dlink"], 1)
                dve.wait_ge(S["dlink"], chain[0])

            V.memset(bias[:, 0:1], math.pi / 2)
            V.memset(bias[:, 1:2], 1.0)
            V.memset(bias[:, 4:5], 1.0 + 1e-6)
            V.memset(bias2[:], EPS)
            V.memset(ones[:], 1.0)
            V.memset(v_all[:], 1.0)
            V.memset(pv, 0.0).then_inc(S["pv_init"], 1)
            dve.wait_ge(S["consts_loaded"], 16 * (len(CONST) + 7))
            link(V.tensor_scalar(tmp1[:, 0:1], tt[:, 1:2], 1e-6, None, ALU.add))
            link(V.reciprocal(tmp1[:, 1:2], tmp1[:, 0:1]))
            V.tensor_scalar(bias[:, 2:3], tmp1[:, 1:2], -1.0, None, ALU.mult)
            V.tensor_tensor(bias[:, 3:4], tmp1[:, 1:2], tt[:, 0:1], ALU.mult)
            link(V.tensor_scalar(bqs[:], bqk[:, 0:1], 1.0 / math.sqrt(HD), None, ALU.mult))
            for i in range(3):
                last = V.tensor_scalar(ang[:, i, :], pos[:, i, :], ph[:, i:i + 1], None, ALU.add)
            link(last)
            link(V.tensor_scalar(rnd[:], ang[:], 1.0 / TWO_PI, MAGIC, ALU.mult, ALU.add))
            link(V.tensor_scalar(rnd[:], rnd[:], -MAGIC, None, ALU.add))
            link(V.scalar_tensor_tensor(ang[:], rnd[:], -C1, ang[:], ALU.mult, ALU.add))
            link(V.scalar_tensor_tensor(ang[:], rnd[:], -C2, ang[:], ALU.mult, ALU.add))
            link(V.tensor_scalar(ang[:], ang[:], 3.1415925, -3.1415925, ALU.min, ALU.max))
            link(V.tensor_scalar(aby[:], ang[:], -1.0, None, ALU.mult))
            link(V.tensor_tensor(aby[:], aby[:], ang[:], ALU.max))
            V.tensor_copy(tmp1[:, 2:3], tmp1[:, 1:2]).then_inc(S["trig_ready"], 1)
            dve.wait_ge(S["sincos_ready"], 1)
            cb, sbb = pos[:, 3, :], pos[:, 4, :]
            V.tensor_copy(fk[:, 0, :], cs[:, 1, :])
            V.tensor_copy(gq[:, 0, :], sn[:, 0, :])
            V.tensor_tensor(fk[:, 1, :], sn[:, 1, :], cb, ALU.mult)
            V.tensor_copy(gq[:, 1, :], cs[:, 2, :])
            V.scalar_tensor_tensor(fk[:, 2, :], sn[:, 1, :], -1.0, sbb, ALU.mult, ALU.mult)
            V.tensor_copy(gq[:, 2, :], sn[:, 2, :])
            V.tensor_copy(fk[:, 3, :], cb)
            V.tensor_tensor(gq[:, 3, :], sn[:, 2, :], cs[:, 0, :], ALU.mult)
            V.tensor_copy(fk[:, 4, :], sbb)
            V.tensor_tensor(gq[:, 4, :], cs[:, 2, :], cs[:, 0, :], ALU.mult).then_inc(S["factors_ready"], 1)
            V.tensor_copy(tmp1[:, 2:3], tmp1[:, 0:1]).then_inc(S["cast"], 1)

            def project(g):
                for i in range(2):
                    b = 2 * g + i
                    dve.wait_ge(S["v_ready"], b + 1)
                    V.tensor_tensor(
                        v_all[:, :, bass.ds(4 * b, 4), 0:HD].rearrange("p h c d -> p c h d"),
                        sm[i].rearrange("p (c h d) -> p c h d", c=4, h=NH),
                        bvb[:].rearrange("p (h d) -> p h d", h=NH).unsqueeze(1).broadcast_to([P, 4, NH, HD]),
                        ALU.add).then_inc(S["v_used"], 1)
                    dve.wait_ge(S["evac_done"], b + 1)
                    V.tensor_tensor(qkr[i], qkf[i], parts[i][:, 0], ALU.subtract).then_inc(S["split_step"], 1)
                    dve.wait_ge(S["split_step"], 2 * b + 1)
                    V.tensor_copy(parts[i][:, 1], qkr[i]).then_inc(S["split_step"], 1)
                    dve.wait_ge(S["split_step"], 2 * b + 2)
                    V.tensor_tensor(parts[i][:, 2], qkr[i], parts[i][:, 1], ALU.subtract).then_inc(S["split_done"], 1)

            loop(dve, 0, 4, project, False)

            def row_max(r, c16, k):
                dve.wait_ge(S["sm_ready"], k + 1)
                ins = V.tensor_reduce(neg_max[:, r, c16:c16 + 1], sm[c16 % 2], AX.X, ALU.max, negate=True)
                ins.then_inc(S["sm_done"], 1)
                return ins

            def split_max(r, u):
                dve.wait_ge(S["mt_ready"], u + 1)
                V.tensor_copy(m_parts[:, r, 0, :], misc[0:16, 0:P]).then_inc(S["msub"], 1)
                dve.wait_ge(S["msub"], u + 1)
                V.tensor_tensor(m_parts[:, r, 1, :], misc[0:16, 0:P], m_parts[:, r, 0, :], ALU.subtract
                                ).then_inc(S["mt_used"], 1)

            def all_max(u):
                dve.wait_ge(S["sm_done"], 16 * (u + 1))
                V.tensor_copy(tmp1[:, 2:3], tmp1[:, 1:2]).then_inc(S["max_ready"], 1)

            def clamp(w, par):
                dve.wait_ge(S["val_used"], 2 * w + 2)
                V.tensor_scalar(e_buf[par][:], e_buf[par][:], 1e18, None, ALU.min).then_inc(S["clamp_done"], 1)

            def difference(w, par):
                dve.wait_ge(S["ln_done"], w + 1)
                V.tensor_tensor(l_buf[:], l_buf[:], e_buf[par][:], ALU.subtract).then_inc(S["sub_done"], 1)

            for w in range(3):
                clamp(w, w % 2)
                if w < 2:
                    difference(w, w % 2)
            for k in range(32):
                row_max(k // 16, k % 16, k)
                if k % 16 == 15:
                    all_max(k // 16)
            split_max(0, 0)

            def apply_mask(kc, n, hpar, mr):
                dve.wait_ge(S["exp_done"], 2 * n + 2)
                dve.wait_ge(S["mask_ready"], mr)
                k = QB - POOL_B
                pb = probs[kc][:, POOL_B * L:QB * L].rearrange("p (b t) -> p b t", b=k)
                V.tensor_tensor(pb, pb, mask[hpar][:, kc, :].unsqueeze(1).broadcast_to([P, k, L]), ALU.mult
                                ).then_inc(S["dve_mul"], 1)

            def attend(g):
                peeled = isinstance(g, int)
                for r in range(4):
                    u = 4 * g + r
                    for kc in range(KC):
                        n = 4 * u + kc
                        if kc == 0 and not (peeled and u == NU - 1):
                            split_max((r + 1) % 4, u + 1)
                        if not (peeled and u >= NU - 2):
                            for c in range(2):
                                row_max((r + 2) % 4, 4 * kc + c, 16 * (u + 2) + 4 * kc + c)
                        if not (peeled and n == 0):
                            pr = r if kc else r - 1
                            apply_mask((kc + 3) % 4, n - 1, (pr // 2) % 2,
                                       2 * (2 * g + pr // 2) + ((kc + 3) % 4) // 2 + 1)
                        if not (peeled and u >= NU - 2):
                            for c in range(2, 4):
                                row_max((r + 2) % 4, 4 * kc + c, 16 * (u + 2) + 4 * kc + c)
                            if kc == 3:
                                all_max(u + 2)
                        if kc == 1 and not (peeled and u + 2 >= NU):
                            difference(u + 2, r % 2)
                        if kc == 3 and not (peeled and u + 3 >= NU):
                            clamp(u + 3, (r + 1) % 2)

            loop(dve, 0, NU // 4, attend, True)
            apply_mask(3, NU * KC - 1, 1, 2 * NH)

            def residual(b):
                dve.wait_ge(S["y_ready"], b + 1)
                V.tensor_tensor(resid[:, 4 * b:4 * b + 4, :], st[b % 2][:, L:2 * L].rearrange("p (c d) -> p c d", c=4),
                                xbo[:, 4 * b:4 * b + 4, :], ALU.add).then_inc(S["resid_ready"], 1)
                dve.wait_ge(S["resid_ready"], b + 1)
                for t in range(4 * b, 4 * b + 4):
                    V.bn_stats(stats[:, t, :], resid[:, t, :]).then_inc(S["stats_done"], 1)

            dve.wait_ge(S["xbo_ready"], 1)
            dve.wait_ge(S["den_loaded"], 16)
            V.reciprocal(rden, den).then_inc(S["rden_ready"], 1)
            for b in range(B):
                i = b % 2
                dve.wait_ge(s2["oT_loaded"][i], 16 * (b // 2 + 1))
                dve.wait_ge(S["bc_ready"], b + 1)
                wait(dve, S["y_ready"], b - 1)
                V.tensor_tensor(aT[i], st[i][:, 0:L], oT[i], ALU.mult).then_inc(S["aT_ready"], 1)
                if b:
                    residual(b - 1)
            residual(B - 1)
            dve.wait_ge(S["stats_done"], NT)
            for t in range(NT):
                last = V.bn_aggr(mv[:, t, :], stats[:, t, :])
            last.then_inc(S["mv_done"], 1)
            dve.wait_ge(S["sd_ready"], 1)
            link(V.reciprocal(rstd[:], sd[:]))
            for t in range(NT):
                V.tensor_scalar(xa[0][:, t, 0:H], resid[:, t, :], mv[:, t, 0:1], rstd[:, t:t + 1],
                                ALU.subtract, ALU.mult).then_inc(S["x1_ready"], 1)
            link(V.memset(zer, 0.0))
            for s in range(2):
                V.tensor_copy(xa[s][:, :, H].bitcast(I32), destc[:, s, :])
            dve.wait_ge(S["logit_ready"], 1)
            link(V.tensor_tensor(lg, pv[:, 0:NT * NE].rearrange("p (t e) -> p t e", e=NE),
                                 bgb[:].unsqueeze(1).broadcast_to([P, NT, NE]), ALU.add))
            for t in range(NT):
                last = V.max(mx[:, t, :], lg[:, t, :])
            link(last)
            V.tensor_tensor(dlt[:], mx[:, :, 1], mx[:, :, 0], ALU.subtract).then_inc(S["rw_ready"], 1)
            for t in range(NT):
                last = V.max_index(ix[:, t, :], mx[:, t, :], lg[:, t, :])
            link(last)
            link(V.tensor_copy(ixf[:], ix[:, :, 0:2]))
            for s in range(2):
                last = V.tensor_tensor(oh[s], iota8[:].unsqueeze(1).broadcast_to([P, NT, NE]),
                                       ixf[:, :, s].unsqueeze(2).broadcast_to([P, NT, NE]), ALU.is_equal)
            link(last)
            V.tensor_tensor(asg, oh[0], oh[1], ALU.add).then_inc(S["count_ready"], 1)
            dve.wait_ge(S["slots_ready"], 1)
            before = misc[:, 0:256].rearrange("p (e t) -> p e t", e=NE)
            total = misc[:, 256:512]
            link(V.tensor_tensor_scan(inc.rearrange("p e t -> p (e t)"), zer, total, 0.0, ALU.add, ALU.add))
            link(V.tensor_tensor(exc.rearrange("p e t -> p (e t)"), inc.rearrange("p e t -> p (e t)"), total,
                                 ALU.subtract))
            link(V.tensor_tensor(cnt[:], inc[:, :, NT - 1], exc[:, :, 0], ALU.subtract))
            link(V.tensor_scalar(cnti[:], cnt[:], float(P - 1), None, ALU.add))
            link(V.tensor_scalar(cnti[:], cnti[:], 7, None, ALU.arith_shift_right))
            link(V.tensor_copy(tls[:], cnti[:]))
            link(V.tensor_tensor_scan(cumt[:], zer[:, 0:NE], tls[:], 0.0, ALU.add, ALU.add))
            link(V.tensor_tensor(base[:], cumt[:], tls[:], ALU.subtract))
            link(V.scalar_tensor_tensor(base[:], base[:], float(P), exc[:, :, 0], ALU.mult, ALU.subtract))
            link(V.tensor_tensor(posn, before, exc, ALU.add))
            link(V.tensor_tensor(posn, posn, base[:].unsqueeze(2).broadcast_to([P, NE, NT]), ALU.add))
            for s in range(2):
                link(V.tensor_tensor(psel, oh[s], posn.rearrange("p e t -> p t e"), ALU.mult))
                link(V.tensor_reduce(slotf[:, s, :], psel, AX.X, ALU.add))
            link(V.tensor_copy(slot[:], slotf[:]))
            dve.wait_ge(S["edelta_ready"], 1)
            link(V.tensor_scalar(edp[:], edl[:], 1.0, None, ALU.add))
            link(V.reciprocal(sd[:], edp[:]))
            V.tensor_copy(xa[0][:, :, H + 1], sd[:])
            V.tensor_tensor(xa[1][:, :, H + 1], sd[:], edl[:], ALU.mult).then_inc(S["dest_ready"], 1)
            link(V.tensor_tensor(cmp, iotat[:].unsqueeze(2).broadcast_to([P, ET, NE]),
                                 cumt[:].unsqueeze(1).broadcast_to([P, ET, NE]), ALU.is_ge))
            link(V.tensor_reduce(tef[:], cmp, AX.X, ALU.add))
            link(V.tensor_scalar(tef[:], tef[:], float(NE - 1), None, ALU.min))
            V.tensor_copy(te[:], tef[:]).then_inc(S["tiles_ready"], 1)

            ub = [banks[0][:, 512:1024], banks[1][:, 512:1024]]
            htp = banks[2][:, 512:1024]

            def h_mul(r, i):
                dve.wait_ge(S["silu_done"], i + 1)
                wait(dve, S["hT_ready"], i - 1)
                V.tensor_tensor(hh[r % 2], sg[r % 2], ub[r % 2], ALU.mult).then_inc(S["h_ready"], 1)

            def hT_copy(r, i):
                dve.wait_ge(S["hT_ready"], i + 1)
                wait(dve, S["yt_ready"], i - 1)
                V.tensor_copy(hT[r % 2], htp).then_inc(S["hT_copied"], 1)

            def expert(g):
                peeled = isinstance(g, int)
                for r in range(4):
                    i = 4 * g + r
                    h_mul(r, i)
                    if not (peeled and i < 1):
                        hT_copy((r + 3) % 4, i - 1)

            loop(dve, 0, ET // 4, expert, False)
            hT_copy(3, ET - 1)

            for k in range(4):
                dve.wait_ge(s2["yg_loaded"][k % 2], 32 * (k // 2 + 1))
                zt = z_all[:, 8 * k:8 * k + 8, :]
                link(V.tensor_tensor(zt, yg[k % 2][0], yg[k % 2][1], ALU.add))
                V.tensor_tensor(zt, zt, xa[0][:, 8 * k:8 * k + 8, 0:H], ALU.add).then_inc(S["z_ready"], 1)
                dve.wait_ge(S["z_ready"], k + 1)
                for t in range(8 * k, 8 * k + 8):
                    last = V.bn_stats(stats[:, t, :], z_all[:, t, :])
            link(last)
            for t in range(NT):
                last = V.bn_aggr(mv[:, t, :], stats[:, t, :])
            last.then_inc(S["z_stats"], 1)
            dve.wait_ge(S["sd2_ready"], 1)
            link(V.reciprocal(rstd[:], sd[:]))
            for k in range(4):
                for t in range(8 * k, 8 * k + 8):
                    last = V.tensor_scalar(z_all[:, t, :], z_all[:, t, :], mv[:, t, 0:1], rstd[:, t:t + 1],
                                           ALU.subtract, ALU.mult)
                last.then_inc(S["out_ready"], 1)


def launch_arrays(x, Wq, bq, Wk, bk, Wv, bv, Wo, bo, phase, threshold, temperature, wg, bg, Wgate, Wup, Wdown):
    f = np.float32
    c = np.ascontiguousarray
    p = (np.arange(L, dtype=f) / f(L) * f(TWO_PI)).astype(f).reshape(8, 64)
    half = p * f(0.5)
    pos = np.stack([p, p, half, np.cos(half.astype(np.float64)).astype(f), np.sin(half.astype(np.float64)).astype(f)], 1)
    pos = np.tile(pos, (NH, 1, 1))
    sel = np.zeros((P, B, P), f)
    for h in range(NH):
        for b in range(B):
            sel[h * B + b, b, h * HD:(h + 1) * HD] = 1
    fill = np.zeros((ET * P, XW), f)
    fill.view(np.int32)[:, H] = 2 * T + np.arange(ET * P, dtype=np.int32)
    tok = np.arange(T, dtype=np.int32).reshape(NT, P).T
    return {
        "xT": c(x.reshape(T, H).T), "x_tok": c(x.reshape(T, H)),
        "Wq": c(Wq), "Wk": c(Wk), "Wv": c(Wv), "Wo": c(Wo), "bqk": c(np.stack([bq, bk], 1)),
        "bv": c(bv.reshape(H)), "bo": c(bo.reshape(H)), "bg": c(bg.reshape(NE)),
        "thr": c(threshold.reshape(1)), "temp": c(temperature.reshape(1)),
        "phase": c(np.repeat(phase, 8, axis=0)), "wg": c(wg.T),
        "Wgate": c(Wgate.transpose(2, 0, 1).reshape(P, NE * HID)),
        "Wup": c(Wup.transpose(2, 0, 1).reshape(P, NE * HID)),
        "Wdown": c(Wdown.transpose(2, 0, 1).reshape(4, P, NE, H).transpose(1, 2, 0, 3).reshape(P, NE * HID)),
        "c_ident": np.eye(P, dtype=f), "c_sel": sel, "c_pos": c(pos), "c_fill": fill,
        "c_iota8": np.tile(np.arange(NE, dtype=f), (P, 1)), "c_iotat": np.tile(np.arange(ET, dtype=f), (P, 1)),
        "c_dest": c(np.stack([tok, tok + T], 1)), "c_tri": np.triu(np.ones((P, P), f), 1),
    }


def kernel(**inputs):
    import concourse.bacc as bacc
    from concourse.bass_utils import run_bass_kernel_spmd

    given = {k.split("_", 2)[2]: np.asarray(v) for k, v in inputs.items()}
    arrays = launch_arrays(**given)
    nc = bacc.Bacc("TRN2", target_bir_lowering=False, num_devices=1)
    feeds, aps = {}, {}
    for name, arr in arrays.items():
        feeds[f"in_{name}"] = arr
        aps[name] = nc.dram_tensor(f"in_{name}", arr.shape, mybir.dt.from_np(arr.dtype), kind="ExternalInput").ap()
    out = nc.dram_tensor("out", (T, H), F32, kind="ExternalOutput").ap()
    build(nc, aps, out)
    r = run_bass_kernel_spmd(nc, [feeds], core_ids=[0])
    return r.results[0]["out"].reshape(B, L, H)
```

```python
import math
from contextlib import ExitStack

import numpy as np

import concourse.bass as bass
from concourse import mybir

F32 = mybir.dt.float32
BF16 = mybir.dt.bfloat16
I32 = mybir.dt.int32
U32 = mybir.dt.uint32
ALU = mybir.AluOpType
ACT = mybir.ActivationFunctionType
AX = mybir.AxisListType

P = 128
B, L, H = 8, 512, 128
T = B * L
NH, HD = 16, 8
NE, HID = 8, 512
NT = T // P
QB = 4
NU = NH * (B // QB)
KC = L // P
UC = QB * L
ROWS = 6 * HD
MROW = 64
NF = 5
QK_LOADS = 7 * 16
RING = 4
ET = 2 * T // P + NE
FILLS = 8
XR = 8
XW = H + 2
C_COLS = 2 * P + 5 * 64 + NE + ET
EPS = 1e-5
TPMS = 0.3
TWO_PI = 2.0 * math.pi
C1 = 6.28125
C2 = TWO_PI - C1
MAGIC = 1.5 * 2.0 ** 23
POOL_B = 3


def wait(eng, sem, value):
    if isinstance(value, int) and value <= 0:
        return
    eng.wait_ge(sem, value)


def wait_alone(eng, turn, sem, value):
    wait(eng, sem, value)
    if not isinstance(value, int):
        eng.sem_inc(turn, 1)


def build(nc, a, out):
    ctx = ExitStack()
    with ctx:
        def sb(name, shape, dt=F32):
            return ctx.enter_context(nc.sbuf_tensor(name, shape, dt))

        def sem(name):
            return ctx.enter_context(nc.semaphore(name))

        def dram(name, shape, dt=F32):
            return nc.dram_tensor(name, shape, dt, kind="Internal").ap()

        qk_dram = dram("qk_parts", (3, 2, P, T), BF16)
        f_dram = dram("mask_key_factors", (P, NF, 64))
        g_dram = dram("mask_query_factors", (P, NF, 64))
        o_dram = dram("head_outputs", (NH, HD + 1, T))
        xs_dram = dram("routed_rows", (ET * P, XW))
        y_dram = dram("expert_rows", (2 * T + ET * P, H))

        arena = sb("arena", [P, 16384])
        probs = [arena[:, 2048 * i:2048 * (i + 1)] for i in range(KC)]
        qs = [arena[:, 8192 + 1024 * i:8192 + 1024 * (i + 1)].bitcast(BF16) for i in range(RING)]
        ks = [arena[:, 12288 + 1024 * i:12288 + 1024 * (i + 1)].bitcast(BF16) for i in range(RING)]
        qkf = [arena[:, 1024 + 1024 * i:2048 + 1024 * i].rearrange("p (s t) -> p s t", s=2) for i in range(2)]
        qkr = [arena[:, 3072 + 1024 * i:4096 + 1024 * i].rearrange("p (s t) -> p s t", s=2) for i in range(2)]
        parts = [arena[:, 5120 + 1536 * i:6656 + 1536 * i].bitcast(BF16).rearrange(
            "p (n s t) -> p n s t", n=3, s=2) for i in range(2)]
        XA = NT * XW
        xa = [arena[:, XA * s:XA * (s + 1)].rearrange("p (t c) -> p t c", c=XW) for s in range(2)]
        resid = arena[:, 2 * XA:2 * XA + NT * H].rearrange("p (t c) -> p t c", c=H)
        z_all = arena[:, XA:XA + NT * H].rearrange("p (t c) -> p t c", c=H)
        yg = [[arena[:, 2 * XA + 2048 * i + 1024 * s:2 * XA + 2048 * i + 1024 * (s + 1)].rearrange(
            "p (t c) -> p t c", c=H) for s in range(2)] for i in range(2)]
        R2 = 2 * XA + NT * H
        oT = [arena[:, R2 + 512 * i:R2 + 512 * (i + 1)] for i in range(2)]
        aT = [arena[:, R2 + 1024 + 512 * i:R2 + 1024 + 512 * (i + 1)] for i in range(2)]
        x1T = [arena[:, R2 + 2048 + 512 * i:R2 + 2048 + 512 * (i + 1)] for i in range(2)]

        v_all = sb("v_all", [P, NH, NT, HD + 1])
        spare = v_all[:].rearrange("p h t d -> p (h t d)")
        table = lambda k: spare[:, 256 * k:256 * (k + 1)]
        lg, mx, asg, psel = (table(k).rearrange("p (t e) -> p t e", e=NE) for k in range(4))
        oh = [table(4 + k).rearrange("p (t e) -> p t e", e=NE) for k in range(2)]
        inc, exc, posn = (table(6 + k).rearrange("p (e t) -> p e t", e=NE) for k in range(3))
        ix = table(9).bitcast(U32).rearrange("p (t e) -> p t e", e=NE)
        zer = table(10)
        cmp = spare[:, 11 * 256:11 * 256 + ET * NE].rearrange("p (t e) -> p t e", e=NE)
        xs = [spare[:, 3400 + XW * i:3400 + XW * (i + 1)] for i in range(XR)]
        v_cur = [sb(f"v_cur{i}", [P, NT, HD + 1]) for i in range(2)]
        mask = [sb(f"mask{i}", [P, KC, L]) for i in range(2)]
        sg = [mask[0][:, i, :] for i in range(2)]
        sel = mask[0][:, 0:2, :].rearrange("p k (b c) -> p (k b) c", c=P)
        hh = [mask[0][:, 2 + i, :] for i in range(2)]
        stats = mask[1][:, 2, 0:NT * 6].rearrange("p (t c) -> p t c", c=6)
        mv = mask[1][:, 2, NT * 6:NT * 8].rearrange("p (t c) -> p t c", c=2)
        hT = [mask[1][:, i, :] for i in range(2)]
        e_buf = [sb(f"e_buf{i}", [P, 2, L]) for i in range(2)]
        l_buf = sb("l_buf", [P, 2, L])
        den, rden = e_buf[0][:, 0, :], e_buf[0][:, 1, :]
        l_flat = l_buf[:].rearrange("p i t -> p (i t)")
        yo = [l_flat[:, P * i:P * (i + 1)] for i in range(XR)]
        xT = [e_buf[1][:, 0, P * i:P * (i + 1)] for i in range(2)]
        fac = [sb(f"fac{i}", [NF, 2, 8, 64]) for i in range(2)]
        o_sb = [sb(f"o_sb{i}", [P, L]) for i in range(2)]
        xbo = sb("xbo", [P, NT, H])
        wgate = sb("wgate", [P, NE * HID])
        xb = [wgate[:, b * L:(b + 1) * L] for b in range(B)]
        wup = sb("wup", [P, NE * HID])
        wdown = sb("wdown", [P, NE * HID])
        wqkvo = sb("wqkvo", [P, 4, H])
        bqs = sb("bqs", [P, 1])
        tmp1 = sb("tmp1", [P, 4])
        ang = sb("ang", [P, 3, 64])
        rnd = sb("rnd", [P, 3, 64])
        aby = sb("aby", [P, 3, 64])
        sn = sb("sn", [P, 3, 64])
        cs = sb("cs", [P, 3, 64])
        fk = sb("fk", [P, NF, 64])
        gq = sb("gq", [P, NF, 64])
        bias = sb("bias", [P, 5])
        cpack = sb("cpack", [P, C_COLS])
        ident, tri = cpack[:, 0:P], cpack[:, P:2 * P]
        pos = cpack[:, 2 * P:2 * P + 5 * 64].rearrange("p (k t) -> p k t", k=5)
        iota8, iotat = cpack[:, C_COLS - ET - NE:C_COLS - ET], cpack[:, C_COLS - ET:C_COLS]
        ipack = sb("ipack", [P, 3 + 2 + NE])
        ph, bqk, wr = ipack[:, 0:3], ipack[:, 3:5], ipack[:, 5:5 + NE]
        rows = sb("rows", [P, 2 * H + NE + 2])
        bvb, bob, bgb, tt = rows[:, 0:H], rows[:, H:2 * H], rows[:, 2 * H:2 * H + NE], rows[:, 2 * H + NE:]
        bias2 = sb("bias2", [P, 1])
        neg_max = sb("neg_max", [P, RING, 16])
        m_parts = sb("m_parts", [16, RING, 2, P], BF16)
        sd = sb("sd", [P, NT])
        rstd = sb("rstd", [P, NT])
        ixf = sb("ixf", [P, NT, 2])
        destc = sb("destc", [P, 2, NT], I32)
        ones = sb("ones", [P, P])
        cnt = sb("cnt", [P, NE])
        cnti = sb("cnti", [P, NE], I32)
        tls = sb("tls", [P, NE])
        cumt = sb("cumt", [P, NE])
        base = sb("base", [P, NE])
        slotf = sb("slotf", [P, 2, NT])
        slot = sb("slot", [P, 2, NT], I32)
        tef = sb("tef", [P, ET])
        te = sb("te", [P, ET], I32)
        dlt = sb("dlt", [P, NT])
        edl = sb("edl", [P, NT])
        edp = sb("edp", [P, NT])

        banks = [ctx.enter_context(nc.psum_tensor(f"bank{i}", [P, 1024], F32)) for i in range(4)]
        st = [banks[0], banks[1]]
        sm = [banks[2][:, 0:512], banks[2][:, 512:1024]]
        pv = banks[3][:, 0:512]
        misc = banks[3][:, 512:1024]

        names = """consts_loaded weights_loaded expert_w_loaded trig_ready sincos_ready
        factors_ready proj_ready v_ready evac_done v_used split_step split_done xbo_ready
        st_ready exp_done sm_ready sm_done mt_ready mt_used msub
        val_ready val_used clamp_done ln_done sub_done mask_ready
        v_cur_ready pv_step pv_evac pool_mul dve_mul pv_init x_tok_loaded p1_ready sp_turn pool_turn sel_loaded
        den_loaded rden_ready bc_ready aT_ready y_ready resid_ready stats_done mv_done sd_ready
        x1_ready x1b_ready x1t_ready x1t_copied logit_ready edelta_ready rw_ready count_ready slots_ready
        tiles_ready filled scattered dlink zeroed
        xT_ready xT_copied gu_ready silu_done h_ready hT_ready hT_copied yt_ready yo_ready
        z_ready z_stats sd2_ready out_ready stored dest_ready f_stored """.split()
        S = {n: sem(n) for n in names}
        s2 = {n: [sem(f"{n}{i}") for i in range(k)] for n, k in
              (("x_loaded", B), ("parts_stored", 2), ("qk_loaded", 4), ("m_loaded", 4), ("fac_loaded", 2),
               ("o_stored", 2), ("oT_loaded", 2), ("xs_loaded", XR), ("yg_loaded", 2), ("y_scattered", XR))}

        block = ctx.enter_context(nc.Block())

        def loop(eng, first, last, body, peel_last):
            body(first)
            with eng.Fori(first + 1, last - (1 if peel_last else 0)) as g:
                body(g)
            if peel_last:
                body(last - 1)

        @block.sync
        def _(sp):
            sp.dma_start(xb[0], a["xT"][:, 0:L]).then_inc(s2["x_loaded"][0], 16)
            for t, n in ((ipack, "ipack"), (cpack, "cpack"), (destc, "c_dest")):
                sp.dma_start(t[:], a[n]).then_inc(S["consts_loaded"], 16)
            for b in range(2, B, 2):
                sp.dma_start(xb[b], a["xT"][:, b * L:(b + 1) * L]).then_inc(s2["x_loaded"][b], 16)
            sp.wait_ge(S["factors_ready"], 1)
            sp.dma_start(f_dram, fk[:]).then_inc(S["f_stored"], 16)
            sp.dma_start(g_dram, gq[:]).then_inc(S["f_stored"], 16)
            sp.wait_ge(S["f_stored"], 32)

            def load_fac(slot_, hv):
                for s, dr in ((0, f_dram), (1, g_dram)):
                    sp.dma_start(fac[slot_][:, s], dr[bass.ds(hv * 8, 8)].rearrange("c f t -> f c t")
                                 ).then_inc(s2["fac_loaded"][slot_], 16)

            def load_qk(r, head, q):
                at = 0
                for n in (3, 2, 1):
                    rows = slice(at * HD, (at + n) * HD)
                    sp.dma_start(qs[r][rows, :], qk_dram[3 - n, 0, bass.ds(head * HD, HD), q * UC:(q + 1) * UC]
                                 .unsqueeze(0).broadcast_to([n, HD, UC])).then_inc(s2["qk_loaded"][r], 16)
                    sp.dma_start(ks[r][rows, :], qk_dram[0:n, 1, bass.ds(head * HD, HD), q * UC:(q + 1) * UC]
                                 ).then_inc(s2["qk_loaded"][r], 16)
                    at += n
                sp.dma_start(qs[r][MROW:MROW + 2, :], ks[r][MROW + 2:MROW + 4, :]).then_inc(s2["qk_loaded"][r], 16)

            def store_max(r):
                for n in range(2):
                    sp.dma_start(qs[r][MROW + n:MROW + n + 1, :], m_parts[:, r, n, :]
                                 ).then_inc(s2["m_loaded"][r], 16)

            def store_o(par, head, q):
                for b in range(QB):
                    c = (q * QB + b) * L
                    sp.dma_start(o_dram[bass.ds(head, 1), :, c:c + L], o_sb[par][32 * b:32 * b + HD + 1, :]
                                 ).then_inc(s2["o_stored"][par], 16)

            def store_parts(b):
                sp.wait_ge(S["split_done"], b + 1)
                sp.dma_start(qk_dram[:, :, :, b * L:(b + 1) * L].rearrange("n s p t -> p n s t"),
                             parts[b % 2]).then_inc(s2["parts_stored"][b % 2], 16)

            load_fac(0, 0)
            load_fac(1, 1)
            sp.wait_ge(S["zeroed"], 2)
            for q in range(2):
                for b in range(4 * q, 4 * q + 4):
                    store_parts(b)
                for i in range(2):
                    sp.wait_ge(s2["parts_stored"][i], 16 * 2 * (q + 1))
                load_qk(q, 0, q)
                load_qk(2 + q, 1, q)
            sp.wait_ge(S["v_ready"], B)
            for t, n in ((wgate, "Wgate"), (wup, "Wup"), (wdown, "Wdown")):
                sp.dma_start(t[:], a[n]).then_inc(S["expert_w_loaded"], 16)
            for i in range(FILLS):
                n = ET * P // FILLS
                sp.dma_start(xs_dram[i * n:(i + 1) * n, :], a["c_fill"][i * n:(i + 1) * n, :]
                             ).then_inc(S["filled"], 16)
            sp.dma_start(xbo[:], a["x_tok"].rearrange("(t p) c -> p t c", p=P)).then_inc(S["x_tok_loaded"], 16)
            sp.wait_ge(S["mt_used"], 1)
            store_max(0)

            def attend(g):
                peeled = isinstance(g, int)
                for r in range(4):
                    u = 4 * g + r
                    lastg = peeled and g == NU // 4 - 1
                    if not (lastg and r == 3):
                        wait_alone(sp, S["sp_turn"], S["mt_used"], u + 2)
                        store_max((r + 1) % 4)
                    if not (peeled and u == 0):
                        wait_alone(sp, S["sp_turn"], S["pv_evac"], u)
                        store_o((r + 1) % 2, 2 * g + (r - 1) // 2, (r + 1) % 2)
                    hf = 2 * g + r // 2 + 2
                    if r % 2 == 0 and not (peeled and g == NU // 4 - 1):
                        wait_alone(sp, S["sp_turn"], S["val_ready"], 4 * hf - 4)
                        load_fac((r // 2) % 2, hf)
                    if not lastg:
                        wait_alone(sp, S["sp_turn"], S["st_ready"], 8 * (u + 1))
                        load_qk(r, 2 * (g + 1) + r // 2, r % 2)

            loop(sp, 0, NU // 4, attend, True)
            sp.wait_ge(S["pv_evac"], NU)
            store_o((NU - 1) % 2, NH - 1, 1)
            for i in range(2):
                sp.wait_ge(s2["o_stored"][i], 64 * NU // 2)
            sp.wait_ge(S["pool_mul"], NU * KC)
            sp.wait_ge(S["dve_mul"], NU * KC)
            sp.dma_start(sel, a["c_sel"]).then_inc(S["sel_loaded"], 16)
            sp.dma_start(den, o_dram[:, HD, :].rearrange("h (b t) -> h b t", b=B)).then_inc(S["den_loaded"], 16)

            def load_oT(g):
                for i in range(2):
                    wait_alone(sp, S["sp_turn"], S["aT_ready"], 2 * g + i - 1)
                    sp.dma_start(oT[i], o_dram[:, 0:HD, bass.ds((2 * g + i) * L, L)]
                                 ).then_inc(s2["oT_loaded"][i], 16)

            loop(sp, 0, 4, load_oT, False)
            sp.wait_ge(S["scattered"], 16 * 2 * NT)

            def load_xs(g):
                for r in range(XR):
                    i = XR * g + r
                    wait_alone(sp, S["sp_turn"], s2["y_scattered"][r], 16 * g)
                    sp.dma_start(xs[r], xs_dram[bass.ds(i * P, P), :]).then_inc(s2["xs_loaded"][r], 16)

            loop(sp, 0, ET // XR, load_xs, False)
            for r in range(XR):
                sp.wait_ge(s2["y_scattered"][r], 16 * (ET // XR))
            for k in range(4):
                if k >= 2:
                    wait_alone(sp, S["sp_turn"], S["z_ready"], k - 1)
                for s in range(2):
                    sp.dma_start(yg[k % 2][s], y_dram[s * T + k * 1024:s * T + (k + 1) * 1024, :].rearrange(
                        "(t p) c -> p t c", p=P)).then_inc(s2["yg_loaded"][k % 2], 16)
            for k in range(4):
                wait_alone(sp, S["sp_turn"], S["out_ready"], k + 1)
                sp.dma_start(out[k * 1024:(k + 1) * 1024, :].rearrange("(t p) c -> p t c", p=P),
                             z_all[:, 8 * k:8 * k + 8, :]).then_inc(S["stored"], 16)
            sp.wait_ge(S["stored"], 64)

        @block.tensor
        def _(pe):
            mm = nc.tensor.matmul
            def project(b):
                i = b % 2
                pe.wait_ge(s2["x_loaded"][b], 16)
                wait(pe, S["evac_done"], b - 1)
                for s in range(2):
                    last = mm(st[i][:, s * L:(s + 1) * L], wqkvo[:, s, :], xb[b], start=True, stop=True)
                last.then_inc(S["proj_ready"], 1)
                wait(pe, S["v_used"], b - 1)
                for c in range(4):
                    last = mm(sm[i][:, c * P:(c + 1) * P], xb[b][:, c * P:(c + 1) * P], wqkvo[:, 2, :],
                              start=True, stop=True)
                last.then_inc(S["v_ready"], 1)

            def s_chunk(r, b, c, k):
                pe.wait_ge(S["sm_done"], k - 1) if not (isinstance(k, int) and k < 2) else None
                mm(sm[c % 2], qs[r][:, b * L + c * P:b * L + (c + 1) * P], ks[r][:, b * L:(b + 1) * L],
                   start=True, stop=True).then_inc(S["sm_ready"], 1)

            def turn_max(r, u):
                pe.wait_ge(S["sm_done"], 16 * (u + 1))
                nc.tensor.transpose(misc[0:16, 0:P], neg_max[:, r, :], ident).then_inc(S["mt_ready"], 1)

            def mask_arg(par, kc):
                mm(misc, fac[par][:, 0].rearrange("f c t -> f (c t)")[:, kc * P:(kc + 1) * P],
                   fac[par][:, 1].rearrange("f c t -> f (c t)"), start=True, stop=True
                   ).then_inc(S["val_ready"], 1)

            pe.wait_ge(S["weights_loaded"], 16)
            for b in range(B):
                project(b)
                if b in (3, 5, 7):
                    for v in range(b - 3, b - 1):
                        if v % 4 == 0:
                            pe.wait_ge(s2["fac_loaded"][v // 4], 32)
                        wait(pe, S["val_used"], v)
                        mask_arg(v // 4, v % 4)
            pe.wait_ge(S["evac_done"], B)
            pe.wait_ge(S["v_used"], B)
            for u in range(2):
                pe.wait_ge(s2["qk_loaded"][u], QK_LOADS)
                for k in range(16):
                    s_chunk(u, k // 4, k % 4, 16 * u + k)
            pe.wait_ge(S["val_used"], 6)
            turn_max(0, 0)
            pe.wait_ge(S["pv_init"], 1)

            def sums(par, kc, n, u):
                pe.wait_ge(S["pool_mul"], n + 1)
                pe.wait_ge(S["dve_mul"], n + 1)
                if kc == 0:
                    wait(pe, S["pv_evac"], u)
                hpar, q = par
                for b in range(QB):
                    last = mm(pv[32 * b:32 * b + HD + 1, :], v_cur[hpar][:, (q * QB + b) * KC + kc, :],
                              probs[kc][:, b * L:(b + 1) * L], start=(kc == 0), stop=(kc == KC - 1))
                last.then_inc(S["pv_step"], 1)

            def attend(g):
                peeled = isinstance(g, int)
                for r in range(4):
                    u = 4 * g + r
                    last_s = peeled and u >= NU - 2
                    r2 = (r + 2) % 4
                    for kc in range(KC):
                        n = 4 * u + kc
                        if kc == 0:
                            pe.wait_ge(s2["m_loaded"][r], 32 * (g + 1))
                            if not last_s:
                                pe.wait_ge(s2["qk_loaded"][r2], QK_LOADS * (g + (1 if r < 2 else 2)))
                        for half in range(2):
                            wait(pe, S["exp_done"], 2 * n + half - 1)
                            for i in range(2):
                                b = 2 * half + i
                                last = mm(st[half][:, i * L:(i + 1) * L],
                                          ks[r][:, b * L + kc * P:b * L + (kc + 1) * P],
                                          qs[r][:, b * L:(b + 1) * L], start=True, stop=True)
                            last.then_inc(S["st_ready"], 1)
                            if not last_s:
                                s_chunk(r2, kc, half, 16 * (u + 2) + 4 * kc + half)
                        if kc == 0 and not (peeled and u == NU - 1):
                            wait(pe, S["val_used"], 6 + 2 * u) if not (peeled and u > NU - 4) else None
                            turn_max((r + 1) % 4, u + 1)
                        if kc in (1, 2) and not (peeled and u + 3 >= NU):
                            if kc == 1:
                                pe.wait_ge(S["mt_used"], u + 2)
                                hv = (r + 3) // 2
                                pe.wait_ge(s2["fac_loaded"][hv % 2], 32 * (g + 1 + hv // 2))
                            else:
                                pe.wait_ge(S["val_used"], 6 + 2 * u + 1)
                            mask_arg(((r + 3) // 2) % 2, 2 * ((r + 3) % 2) + kc - 1)
                        if not last_s:
                            s_chunk(r2, kc, 2, 16 * (u + 2) + 4 * kc + 2)
                        if not (peeled and n < 2):
                            pn = (kc + 2) % 4
                            pr = r if kc >= 2 else r - 1
                            if pn == 0 and pr % 2 == 0:
                                pe.wait_ge(S["v_cur_ready"], 2 * g + (pr // 2) + 1)
                            sums((((pr // 2) % 2), pr % 2), pn, n - 2, 4 * g + pr)
                        if not last_s:
                            s_chunk(r2, kc, 3, 16 * (u + 2) + 4 * kc + 3)

            loop(pe, 0, NU // 4, attend, True)
            for n in (NU * KC - 2, NU * KC - 1):
                sums((1, 1), n % 4, n, NU - 1)

            pe.wait_ge(S["consts_loaded"], 64)
            pe.wait_ge(S["rden_ready"], 1)
            pe.wait_ge(S["sel_loaded"], 16)
            for b in range(B):
                i = b % 2
                wait(pe, S["aT_ready"], b - 1)
                mm(st[i][:, 0:L], sel[:, b, :], rden, start=True, stop=True).then_inc(S["bc_ready"], 1)
                pe.wait_ge(S["aT_ready"], b + 1)
                wait(pe, S["resid_ready"], b - 1)
                for c in range(4):
                    last = mm(st[i][:, L + c * P:L + (c + 1) * P], aT[i][:, c * P:(c + 1) * P], wqkvo[:, 3, :],
                              start=True, stop=True)
                last.then_inc(S["y_ready"], 1)
            for b in range(B):
                i = b % 2
                pe.wait_ge(S["x1_ready"], 4 * (b + 1))
                wait(pe, S["x1t_copied"], b - 1)
                for c in range(4):
                    last = nc.tensor.transpose(sm[i][:, c * P:(c + 1) * P], xa[0][:, 4 * b + c, 0:H], ident)
                last.then_inc(S["x1t_ready"], 1)
                pe.wait_ge(S["x1t_copied"], b + 1)
                for c in range(4):
                    t = 4 * b + c
                    last = mm(pv[:, t * NE:(t + 1) * NE], x1T[i][:, c * P:(c + 1) * P], wr,
                              start=True, stop=True)
            last.then_inc(S["logit_ready"], 1)
            pe.wait_ge(S["count_ready"], 1)
            av = asg.rearrange("p t e -> p e t")
            mm(misc[:, 0:256], tri, av, start=True, stop=True)
            mm(misc[:, 256:512], ones[:], av, start=True, stop=True).then_inc(S["slots_ready"], 1)

            gb = [banks[0][:, 0:512], banks[1][:, 0:512]]
            ub = [banks[0][:, 512:1024], banks[1][:, 512:1024]]
            xtp, htp = banks[2][:, 0:512], banks[2][:, 512:1024]
            yp = banks[3]
            pe.wait_ge(S["tiles_ready"], 1)
            pe.wait_ge(S["expert_w_loaded"], 48)

            def turn_x(r, i, g):
                pe.wait_ge(s2["xs_loaded"][r], 16 * (g + 1))
                wait(pe, S["xT_copied"], i)
                nc.tensor.transpose(xtp[:, 0:P], xs[r][:, 0:H], ident).then_inc(S["xT_ready"], 1)

            def expert_of(i):
                return pe.value_load(te[0:1, bass.ds(i, 1)], min_val=0, max_val=(NE - 1) * HID)

            def down(r, i, e):
                pe.wait_ge(S["hT_copied"], i + 1)
                wait(pe, S["yo_ready"], i - 1)
                for c in range(4):
                    last = mm(yp[:, 512 * (r % 2):512 * (r % 2) + H], hT[r % 2][:, c * P:(c + 1) * P],
                              wdown[:, bass.ds(e + c * P, P)], start=(c == 0), stop=(c == 3))
                last.then_inc(S["yt_ready"], 1)

            def turn_h(r, i):
                pe.wait_ge(S["h_ready"], i + 1)
                wait(pe, S["hT_copied"], i)
                for c in range(4):
                    last = nc.tensor.transpose(htp[:, c * P:(c + 1) * P], hh[r % 2][:, c * P:(c + 1) * P], ident)
                last.then_inc(S["hT_ready"], 1)

            turn_x(0, 0, 0)

            def expert(g):
                peeled = isinstance(g, int)
                for r in range(XR):
                    i = XR * g + r
                    e = expert_of(i)
                    e_old = expert_of(i - 2) if not (peeled and i < 2) else None
                    pe.wait_ge(S["xT_copied"], i + 1)
                    wait(pe, S["h_ready"], i - 1)
                    mm(gb[r % 2], xT[r % 2], wgate[:, bass.ds(e, HID)], start=True, stop=True)
                    mm(ub[r % 2], xT[r % 2], wup[:, bass.ds(e, HID)], start=True, stop=True
                       ).then_inc(S["gu_ready"], 1)
                    if not (peeled and i + 1 >= ET):
                        turn_x((r + 1) % XR, i + 1, g + (1 if r == XR - 1 else 0))
                    if not (peeled and i < 2):
                        down((r + 2) % 4, i - 2, e_old)
                    if not (peeled and i < 1):
                        turn_h((r + 3) % 4, i - 1)

            loop(pe, 0, ET // XR, expert, True)
            down(2, ET - 2, expert_of(ET - 2))
            turn_h(3, ET - 1)
            down(3, ET - 1, expert_of(ET - 1))

        @block.scalar
        def _(act):
            A = nc.scalar.activation
            RS = 1.0 / math.sqrt(HD)
            for t, src, m in ((wqkvo, "W", "weights_loaded"), (rows, "rows", "consts_loaded")):
                src = a[src] if src == "W" else a[src].partition_broadcast(P)
                act.dma_start(t[:], src).then_inc(S[m], 16)
            for b in range(1, B, 2):
                act.dma_start(xb[b], a["xT"][:, b * L:(b + 1) * L]).then_inc(s2["x_loaded"][b], 16)
            act.wait_ge(S["trig_ready"], 1)
            A(sn[:], ang[:], ACT.Sin)
            A(cs[:], aby[:], ACT.Sin, bias=bias[:, 0:1], scale=-1.0).then_inc(S["sincos_ready"], 1)
            nc.scalar.preload_act_table_set("natural_log_exp_and_others")

            def project(b):
                i = b % 2
                act.wait_ge(S["proj_ready"], b + 1)
                wait(act, s2["parts_stored"][i], 16 * (b // 2))
                A(qkf[i][:, 0, :], st[i][:, 0:L], ACT.Identity, bias=bqs[:], scale=RS)
                A(parts[i][:, 0, 0, :], st[i][:, 0:L], ACT.Identity, bias=bqs[:], scale=RS)
                A(qkf[i][:, 1, :], st[i][:, L:2 * L], ACT.Identity, bias=bqk[:, 1:2])
                A(parts[i][:, 0, 1, :], st[i][:, L:2 * L], ACT.Identity, bias=bqk[:, 1:2]
                  ).then_inc(S["evac_done"], 1)

            def mask_exp(v, par, i):
                act.wait_ge(S["val_ready"], v + 1)
                A(e_buf[par][:, i, :], misc, ACT.Exp, bias=bias[:, 3:4], scale=bias[:, 2:3]
                  ).then_inc(S["val_used"], 1)

            def mask_ln(w, par):
                act.wait_ge(S["clamp_done"], w + 1)
                wait(act, S["mask_ready"], w)
                A(l_buf[:], e_buf[par][:], ACT.Ln, bias=bias[:, 4:5], scale=1e-6)
                A(e_buf[par][:], e_buf[par][:], ACT.Ln, bias=bias[:, 1:2]).then_inc(S["ln_done"], 1)

            def mask_fin(w, hpar, pair):
                act.wait_ge(S["sub_done"], w + 1)
                A(mask[hpar][:, 2 * pair:2 * pair + 2, :], l_buf[:], ACT.Exp, scale=TPMS).then_inc(S["mask_ready"], 1)

            def take_v(head, par):
                nc.scalar.copy(v_cur[par][:], v_all[:, head]).then_inc(S["v_cur_ready"], 1)

            for b in range(B):
                project(b)
                if b in (3, 5, 7):
                    w = (b - 3) // 2
                    if w == 2:
                        act.wait_ge(S["sub_done"], 1)
                    for i in range(2):
                        mask_exp(2 * w + i, w % 2, i)
                if b in (4, 6):
                    mask_ln((b - 4) // 2, (b - 4) // 2)
                if b in (5, 7):
                    mask_fin((b - 5) // 2, 0, (b - 5) // 2)
            act.wait_ge(S["v_used"], B)
            nc.scalar.copy(v_cur[0][:], v_all[:, 0]).then_inc(S["v_cur_ready"], 1)
            act.wait_ge(S["split_done"], B)
            for i in range(2):
                act.wait_ge(s2["parts_stored"][i], 16 * 4)

            def attend(g):
                peeled = isinstance(g, int)
                for r in range(4):
                    u = 4 * g + r
                    for kc in range(KC):
                        n = 4 * u + kc
                        wait(act, S["pv_step"], n - 3)
                        for half in range(2):
                            act.wait_ge(S["st_ready"], 2 * n + half + 1)
                            A(probs[kc][:, half * 1024:(half + 1) * 1024], st[half][:], ACT.Exp
                              ).then_inc(S["exp_done"], 1)
                            if kc == 2 and half == 0 and not (peeled and u == 0):
                                copy_sums(u - 1, (r + 1) % 2, g, r)
                        if kc == 0 and not (peeled and u + 2 >= NU):
                            mask_ln(u + 2, r % 2)
                        if kc in (1, 2) and not (peeled and u + 3 >= NU):
                            if kc == 1:
                                act.wait_ge(S["sub_done"], u + 2)
                            mask_exp(6 + 2 * u + kc - 1, (r + 1) % 2, kc - 1)
                        if kc == 2 and not (peeled and u + 2 >= NU):
                            if True:
                                hv = (r + 2) // 2
                                wait(act, S["pool_mul"], 8 * (2 * g + hv - 1))
                                wait(act, S["dve_mul"], 8 * (2 * g + hv - 1))
                                mask_fin(u + 2, hv % 2, r % 2)
                        if kc == 3 and r % 2 and not (peeled and u == NU - 1):
                            wait(act, S["pv_step"], 8 * (2 * g + r // 2))
                            take_v(2 * g + r // 2 + 1, (r // 2 + 1) % 2)

            def copy_sums(u, par, g, r):
                act.wait_ge(S["pv_step"], 4 * (u + 1))
                wait(act, s2["o_stored"][par], 64 * (2 * g + (0 if r == 0 else (r - 1) // 2)) if r else 64 * (2 * g - 1))
                nc.scalar.copy(o_sb[par][:], pv).then_inc(S["pv_evac"], 1)

            loop(act, 0, NU // 4, attend, True)
            act.wait_ge(S["pv_step"], NU * KC)
            act.wait_ge(s2["o_stored"][1], 64 * (NU // 2 - 1))
            nc.scalar.copy(o_sb[1][:], pv).then_inc(S["pv_evac"], 1)

            act.wait_ge(S["mv_done"], 1)
            A(sd[:], mv[:, :, 1], ACT.Sqrt, bias=bias2[:]).then_inc(S["sd_ready"], 1)
            for b in range(B):
                act.wait_ge(S["x1t_ready"], b + 1)
                nc.scalar.copy(x1T[b % 2], sm[b % 2]).then_inc(S["x1t_copied"], 1)
                nc.scalar.copy(xa[1][:, 4 * b:4 * b + 4, 0:H], xa[0][:, 4 * b:4 * b + 4, 0:H]
                               ).then_inc(S["x1b_ready"], 1)
            act.wait_ge(S["rw_ready"], 1)
            A(edl[:], dlt[:], ACT.Exp).then_inc(S["edelta_ready"], 1)

            gb = [banks[0][:, 0:512], banks[1][:, 0:512]]
            yp = banks[3]

            def x_copy(r, i):
                act.wait_ge(S["xT_ready"], i + 1)
                wait(act, S["gu_ready"], i - 1)
                nc.scalar.copy(xT[r % 2], banks[2][:, 0:P]).then_inc(S["xT_copied"], 1)

            def y_copy(r, i):
                act.wait_ge(S["yt_ready"], i + 1)
                nc.scalar.mul(yo[r], yp[:, 512 * (r % 2):512 * (r % 2) + H], xs[r][:, H + 1:H + 2]
                              ).then_inc(S["yo_ready"], 1)

            x_copy(0, 0)

            def expert(g):
                peeled = isinstance(g, int)
                for r in range(XR):
                    i = XR * g + r
                    act.wait_ge(S["gu_ready"], i + 1)
                    wait(act, S["h_ready"], i - 1)
                    A(sg[r % 2], gb[r % 2], ACT.Silu).then_inc(S["silu_done"], 1)
                    if not (peeled and i + 1 >= ET):
                        x_copy((r + 1) % XR, i + 1)
                    if not (peeled and i < 2):
                        y_copy((r - 2) % XR, i - 2)

            loop(act, 0, ET // XR, expert, True)
            y_copy(XR - 2, ET - 2)
            y_copy(XR - 1, ET - 1)
            act.wait_ge(S["z_stats"], 1)
            A(sd[:], mv[:, :, 1], ACT.Sqrt, bias=bias2[:]).then_inc(S["sd2_ready"], 1)

        @block.gpsimd
        def _(pool):
            for i in range(RING):
                nc.gpsimd.memset(arena[:, 8192 + 1024 * i:8192 + 1024 * (i + 1)], 0.0)
                last = nc.gpsimd.memset(arena[:, 12288 + 1024 * i:12288 + 1024 * (i + 1)], 0.0)
            last.then_inc(S["zeroed"], 1)
            pool.wait_ge(S["zeroed"], 1)
            for i in range(RING):
                last = nc.gpsimd.memset(ks[i][MROW:MROW + 2, :], 1.0)
            last.then_inc(S["zeroed"], 1)
            pool.wait_ge(S["zeroed"], 2)
            pool.wait_ge(S["consts_loaded"], 64)
            for b in range(B):
                pool.wait_ge(S["p1_ready"], b + 1)
                nc.gpsimd.tensor_tensor(parts[b % 2][:, 2], qkr[b % 2], parts[b % 2][:, 1], ALU.subtract
                                        ).then_inc(S["split_done"], 1)

            def attend(g):
                for r in range(4):
                    for kc in range(KC):
                        n = 4 * (4 * g + r) + kc
                        pool.wait_ge(S["exp_done"], 2 * n + 2)
                        pool.wait_ge(S["mask_ready"], 2 * (2 * g + r // 2) + kc // 2 + 1)
                        pb = probs[kc][:, 0:POOL_B * L].rearrange("p (b t) -> p b t", b=POOL_B)
                        nc.gpsimd.tensor_tensor(
                            pb, pb, mask[r // 2][:, kc, :].unsqueeze(1).broadcast_to([P, POOL_B, L]), ALU.mult
                        ).then_inc(S["pool_mul"], 1)

            loop(pool, 0, NU // 4, attend, False)
            pool.wait_ge(S["x_tok_loaded"], 16)
            for b in range(B):
                xbb = xbo[:, 4 * b:4 * b + 4, :]
                nc.gpsimd.tensor_tensor(xbb, xbb, bob.unsqueeze(1).broadcast_to([P, 4, H]), ALU.add
                                        ).then_inc(S["xbo_ready"], 1)
            pool.wait_ge(S["filled"], 16 * (FILLS))
            pool.wait_ge(S["dest_ready"], 1)
            pool.wait_ge(S["x1b_ready"], B)
            for s in range(2):
                for t in range(NT):
                    nc.gpsimd.indirect_dma_start(
                        xs_dram, bass.IndirectOffsetOnAxis(ap=slot[:, s, t:t + 1].bitcast(U32), axis=0),
                        xa[s][:, t, :], None).then_inc(S["scattered"], 16)

            def expert(g):
                for r in range(XR):
                    i = XR * g + r
                    wait_alone(pool, S["pool_turn"], S["yo_ready"], i + 1)
                    nc.gpsimd.indirect_dma_start(
                        y_dram, bass.IndirectOffsetOnAxis(ap=xs[r][:, H:H + 1].bitcast(U32), axis=0),
                        yo[r], None).then_inc(s2["y_scattered"][r], 16)

            loop(pool, 0, ET // XR, expert, False)

        @block.vector
        def _(dve):
            V = nc.vector
            chain = [0]

            def link(ins):
                chain[0] += 1
                ins.then_inc(S["dlink"], 1)
                dve.wait_ge(S["dlink"], chain[0])

            V.memset(bias[:, 0:1], math.pi / 2)
            V.memset(bias[:, 1:2], 1.0)
            V.memset(bias[:, 4:5], 1.0 + 1e-6)
            V.memset(bias2[:], EPS)
            V.memset(ones[:], 1.0)
            V.memset(v_all[:, :, :, HD], 1.0)
            V.memset(pv, 0.0).then_inc(S["pv_init"], 1)
            dve.wait_ge(S["consts_loaded"], 64)
            link(V.tensor_scalar(tmp1[:, 0:1], tt[:, 1:2], 1e-6, None, ALU.add))
            link(V.reciprocal(tmp1[:, 1:2], tmp1[:, 0:1]))
            V.tensor_scalar(bias[:, 2:3], tmp1[:, 1:2], -1.0, None, ALU.mult)
            V.tensor_tensor(bias[:, 3:4], tmp1[:, 1:2], tt[:, 0:1], ALU.mult)
            link(V.tensor_scalar(bqs[:], bqk[:, 0:1], 1.0 / math.sqrt(HD), None, ALU.mult))
            for i in range(3):
                last = V.tensor_scalar(ang[:, i, :], pos[:, i, :], ph[:, i:i + 1], None, ALU.add)
            link(last)
            link(V.tensor_scalar(rnd[:], ang[:], 1.0 / TWO_PI, MAGIC, ALU.mult, ALU.add))
            link(V.tensor_scalar(rnd[:], rnd[:], -MAGIC, None, ALU.add))
            link(V.scalar_tensor_tensor(ang[:], rnd[:], -C1, ang[:], ALU.mult, ALU.add))
            link(V.scalar_tensor_tensor(ang[:], rnd[:], -C2, ang[:], ALU.mult, ALU.add))
            link(V.tensor_scalar(ang[:], ang[:], 3.1415925, -3.1415925, ALU.min, ALU.max))
            link(V.tensor_scalar(aby[:], ang[:], -1.0, None, ALU.mult))
            link(V.tensor_tensor(aby[:], aby[:], ang[:], ALU.max))
            V.tensor_copy(tmp1[:, 2:3], tmp1[:, 1:2]).then_inc(S["trig_ready"], 1)
            dve.wait_ge(S["sincos_ready"], 1)
            cb, sbb = pos[:, 3, :], pos[:, 4, :]
            V.tensor_copy(fk[:, 0, :], cs[:, 1, :])
            V.tensor_copy(gq[:, 0, :], sn[:, 0, :])
            V.tensor_tensor(fk[:, 1, :], sn[:, 1, :], cb, ALU.mult)
            V.tensor_copy(gq[:, 1, :], cs[:, 2, :])
            V.scalar_tensor_tensor(fk[:, 2, :], sn[:, 1, :], -1.0, sbb, ALU.mult, ALU.mult)
            V.tensor_copy(gq[:, 2, :], sn[:, 2, :])
            V.tensor_copy(fk[:, 3, :], cb)
            V.tensor_tensor(gq[:, 3, :], sn[:, 2, :], cs[:, 0, :], ALU.mult)
            V.tensor_copy(fk[:, 4, :], sbb)
            V.tensor_tensor(gq[:, 4, :], cs[:, 2, :], cs[:, 0, :], ALU.mult).then_inc(S["factors_ready"], 1)

            def project(b):
                i = b % 2
                dve.wait_ge(S["v_ready"], b + 1)
                V.tensor_tensor(
                    v_all[:, :, 4 * b:4 * b + 4, 0:HD].rearrange("p h c d -> p c h d"),
                    sm[i].rearrange("p (c h d) -> p c h d", c=4, h=NH),
                    bvb.rearrange("p (h d) -> p h d", h=NH).unsqueeze(1).broadcast_to([P, 4, NH, HD]),
                    ALU.add).then_inc(S["v_used"], 1)
                dve.wait_ge(S["evac_done"], b + 1)
                wait(dve, S["split_done"], b - 1)
                V.tensor_tensor(qkr[i], qkf[i], parts[i][:, 0], ALU.subtract).then_inc(S["split_step"], 1)
                dve.wait_ge(S["split_step"], b + 1)
                V.tensor_copy(parts[i][:, 1], qkr[i]).then_inc(S["p1_ready"], 1)

            def row_max(r, c16, k):
                dve.wait_ge(S["sm_ready"], k + 1)
                V.tensor_reduce(neg_max[:, r, c16:c16 + 1], sm[c16 % 2], AX.X, ALU.max, negate=True
                                ).then_inc(S["sm_done"], 1)

            def split_max(r, u):
                dve.wait_ge(S["mt_ready"], u + 1)
                V.tensor_copy(m_parts[:, r, 0, :], misc[0:16, 0:P]).then_inc(S["msub"], 1)
                dve.wait_ge(S["msub"], u + 1)
                V.tensor_tensor(m_parts[:, r, 1, :], misc[0:16, 0:P], m_parts[:, r, 0, :], ALU.subtract
                                ).then_inc(S["mt_used"], 1)

            def clamp(w, par):
                dve.wait_ge(S["val_used"], 2 * w + 2)
                V.tensor_scalar(e_buf[par][:], e_buf[par][:], 1e18, None, ALU.min).then_inc(S["clamp_done"], 1)

            def difference(w, par):
                dve.wait_ge(S["ln_done"], w + 1)
                V.tensor_tensor(l_buf[:], l_buf[:], e_buf[par][:], ALU.subtract).then_inc(S["sub_done"], 1)

            for b in range(B):
                project(b)
                if b in (3, 5, 7):
                    clamp((b - 3) // 2, (b - 3) // 2 % 2)
                if b in (4, 6):
                    difference((b - 4) // 2, (b - 4) // 2)
            for k in range(32):
                row_max(k // 16, k % 16, k)
            split_max(0, 0)

            def apply_mask(kc, n, hpar, mr):
                dve.wait_ge(S["exp_done"], 2 * n + 2)
                dve.wait_ge(S["mask_ready"], mr)
                k = QB - POOL_B
                pb = probs[kc][:, POOL_B * L:QB * L].rearrange("p (b t) -> p b t", b=k)
                V.tensor_tensor(pb, pb, mask[hpar][:, kc, :].unsqueeze(1).broadcast_to([P, k, L]), ALU.mult
                                ).then_inc(S["dve_mul"], 1)

            def attend(g):
                peeled = isinstance(g, int)
                for r in range(4):
                    u = 4 * g + r
                    for kc in range(KC):
                        n = 4 * u + kc
                        if kc == 0 and not (peeled and u == NU - 1):
                            split_max((r + 1) % 4, u + 1)
                        if not (peeled and u >= NU - 2):
                            for c in range(2):
                                row_max((r + 2) % 4, 4 * kc + c, 16 * (u + 2) + 4 * kc + c)
                        if not (peeled and n == 0):
                            pr = r if kc else r - 1
                            apply_mask((kc + 3) % 4, n - 1, (pr // 2) % 2,
                                       2 * (2 * g + pr // 2) + ((kc + 3) % 4) // 2 + 1)
                        if not (peeled and u >= NU - 2):
                            for c in range(2, 4):
                                row_max((r + 2) % 4, 4 * kc + c, 16 * (u + 2) + 4 * kc + c)
                        if kc == 1 and not (peeled and u + 2 >= NU):
                            difference(u + 2, r % 2)
                        if kc == 3 and not (peeled and u + 3 >= NU):
                            clamp(u + 3, (r + 1) % 2)

            loop(dve, 0, NU // 4, attend, True)
            apply_mask(3, NU * KC - 1, 1, 2 * NH)

            def residual(b):
                dve.wait_ge(S["y_ready"], b + 1)
                dve.wait_ge(S["xbo_ready"], b + 1)
                V.tensor_tensor(resid[:, 4 * b:4 * b + 4, :], st[b % 2][:, L:2 * L].rearrange("p (c d) -> p c d", c=4),
                                xbo[:, 4 * b:4 * b + 4, :], ALU.add).then_inc(S["resid_ready"], 1)
                dve.wait_ge(S["resid_ready"], b + 1)
                for t in range(4 * b, 4 * b + 4):
                    V.bn_stats(stats[:, t, :], resid[:, t, :]).then_inc(S["stats_done"], 1)

            dve.wait_ge(S["den_loaded"], 16)
            V.reciprocal(rden, den).then_inc(S["rden_ready"], 1)
            for b in range(B):
                i = b % 2
                dve.wait_ge(s2["oT_loaded"][i], 16 * (b // 2 + 1))
                dve.wait_ge(S["bc_ready"], b + 1)
                wait(dve, S["y_ready"], b - 1)
                V.tensor_tensor(aT[i], st[i][:, 0:L], oT[i], ALU.mult).then_inc(S["aT_ready"], 1)
                if b:
                    residual(b - 1)
            residual(B - 1)
            dve.wait_ge(S["stats_done"], NT)
            for t in range(NT):
                last = V.bn_aggr(mv[:, t, :], stats[:, t, :])
            last.then_inc(S["mv_done"], 1)
            dve.wait_ge(S["sd_ready"], 1)
            link(V.reciprocal(rstd[:], sd[:]))
            for t in range(NT):
                V.tensor_scalar(xa[0][:, t, 0:H], resid[:, t, :], mv[:, t, 0:1], rstd[:, t:t + 1],
                                ALU.subtract, ALU.mult).then_inc(S["x1_ready"], 1)
            link(V.memset(zer, 0.0))
            for s in range(2):
                V.tensor_copy(xa[s][:, :, H].bitcast(I32), destc[:, s, :])
            dve.wait_ge(S["logit_ready"], 1)
            link(V.tensor_tensor(lg, pv[:, 0:NT * NE].rearrange("p (t e) -> p t e", e=NE),
                                 bgb.unsqueeze(1).broadcast_to([P, NT, NE]), ALU.add))
            for t in range(NT):
                last = V.max(mx[:, t, :], lg[:, t, :])
            link(last)
            V.tensor_tensor(dlt[:], mx[:, :, 1], mx[:, :, 0], ALU.subtract).then_inc(S["rw_ready"], 1)
            for t in range(NT):
                last = V.max_index(ix[:, t, :], mx[:, t, :], lg[:, t, :])
            link(last)
            link(V.tensor_copy(ixf[:], ix[:, :, 0:2]))
            for s in range(2):
                last = V.tensor_tensor(oh[s], iota8.unsqueeze(1).broadcast_to([P, NT, NE]),
                                       ixf[:, :, s].unsqueeze(2).broadcast_to([P, NT, NE]), ALU.is_equal)
            link(last)
            V.tensor_tensor(asg, oh[0], oh[1], ALU.add).then_inc(S["count_ready"], 1)
            dve.wait_ge(S["slots_ready"], 1)
            before = misc[:, 0:256].rearrange("p (e t) -> p e t", e=NE)
            total = misc[:, 256:512]
            link(V.tensor_tensor_scan(inc.rearrange("p e t -> p (e t)"), zer, total, 0.0, ALU.add, ALU.add))
            link(V.tensor_tensor(exc.rearrange("p e t -> p (e t)"), inc.rearrange("p e t -> p (e t)"), total,
                                 ALU.subtract))
            link(V.tensor_tensor(cnt[:], inc[:, :, NT - 1], exc[:, :, 0], ALU.subtract))
            link(V.tensor_scalar(cnti[:], cnt[:], float(P - 1), None, ALU.add))
            link(V.tensor_scalar(cnti[:], cnti[:], 7, None, ALU.arith_shift_right))
            link(V.tensor_copy(tls[:], cnti[:]))
            link(V.tensor_tensor_scan(cumt[:], zer[:, 0:NE], tls[:], 0.0, ALU.add, ALU.add))
            link(V.tensor_tensor(base[:], cumt[:], tls[:], ALU.subtract))
            link(V.scalar_tensor_tensor(base[:], base[:], float(P), exc[:, :, 0], ALU.mult, ALU.subtract))
            link(V.tensor_tensor(posn, before, exc, ALU.add))
            link(V.tensor_tensor(posn, posn, base[:].unsqueeze(2).broadcast_to([P, NE, NT]), ALU.add))
            for s in range(2):
                link(V.tensor_tensor(psel, oh[s], posn.rearrange("p e t -> p t e"), ALU.mult))
                link(V.tensor_reduce(slotf[:, s, :], psel, AX.X, ALU.add))
            link(V.tensor_copy(slot[:], slotf[:]))
            dve.wait_ge(S["edelta_ready"], 1)
            link(V.tensor_scalar(edp[:], edl[:], 1.0, None, ALU.add))
            link(V.reciprocal(sd[:], edp[:]))
            V.tensor_copy(xa[0][:, :, H + 1], sd[:])
            V.tensor_tensor(xa[1][:, :, H + 1], sd[:], edl[:], ALU.mult).then_inc(S["dest_ready"], 1)
            link(V.tensor_tensor(cmp, iotat.unsqueeze(2).broadcast_to([P, ET, NE]),
                                 cumt[:].unsqueeze(1).broadcast_to([P, ET, NE]), ALU.is_ge))
            link(V.tensor_reduce(tef[:], cmp, AX.X, ALU.add))
            link(V.tensor_scalar(tef[:], tef[:], float(NE - 1), float(HID), ALU.min, ALU.mult))
            V.tensor_copy(te[:], tef[:]).then_inc(S["tiles_ready"], 1)

            ub = [banks[0][:, 512:1024], banks[1][:, 512:1024]]
            htp = banks[2][:, 512:1024]

            def h_mul(r, i):
                dve.wait_ge(S["silu_done"], i + 1)
                wait(dve, S["hT_ready"], i - 1)
                V.tensor_tensor(hh[r % 2], sg[r % 2], ub[r % 2], ALU.mult).then_inc(S["h_ready"], 1)

            def hT_copy(r, i):
                dve.wait_ge(S["hT_ready"], i + 1)
                wait(dve, S["yt_ready"], i - 1)
                V.tensor_copy(hT[r % 2], htp).then_inc(S["hT_copied"], 1)

            def expert(g):
                peeled = isinstance(g, int)
                for r in range(XR):
                    i = XR * g + r
                    h_mul(r, i)
                    if not (peeled and i < 1):
                        hT_copy((r + 3) % 4, i - 1)

            loop(dve, 0, ET // XR, expert, False)
            hT_copy(3, ET - 1)

            for k in range(4):
                dve.wait_ge(s2["yg_loaded"][k % 2], 32 * (k // 2 + 1))
                zt = z_all[:, 8 * k:8 * k + 8, :]
                link(V.tensor_tensor(zt, yg[k % 2][0], yg[k % 2][1], ALU.add))
                V.tensor_tensor(zt, zt, xa[0][:, 8 * k:8 * k + 8, 0:H], ALU.add).then_inc(S["z_ready"], 1)
                dve.wait_ge(S["z_ready"], k + 1)
                for t in range(8 * k, 8 * k + 8):
                    last = V.bn_stats(stats[:, t, :], z_all[:, t, :])
            link(last)
            for t in range(NT):
                last = V.bn_aggr(mv[:, t, :], stats[:, t, :])
            last.then_inc(S["z_stats"], 1)
            dve.wait_ge(S["sd2_ready"], 1)
            link(V.reciprocal(rstd[:], sd[:]))
            for k in range(4):
                for t in range(8 * k, 8 * k + 8):
                    last = V.tensor_scalar(z_all[:, t, :], z_all[:, t, :], mv[:, t, 0:1], rstd[:, t:t + 1],
                                           ALU.subtract, ALU.mult)
                last.then_inc(S["out_ready"], 1)


def launch_arrays(x, Wq, bq, Wk, bk, Wv, bv, Wo, bo, phase, threshold, temperature, wg, bg, Wgate, Wup, Wdown):
    f = np.float32
    c = np.ascontiguousarray
    p = (np.arange(L, dtype=f) / f(L) * f(TWO_PI)).astype(f).reshape(8, 64)
    half = p * f(0.5)
    pos = np.stack([p, p, half, np.cos(half.astype(np.float64)).astype(f), np.sin(half.astype(np.float64)).astype(f)], 1)
    pos = np.tile(pos, (NH, 1, 1))
    sel = np.zeros((P, B, P), f)
    for h in range(NH):
        for b in range(B):
            sel[h * B + b, b, h * HD:(h + 1) * HD] = 1
    fill = np.zeros((ET * P, XW), f)
    fill.view(np.int32)[:, H] = 2 * T + np.arange(ET * P, dtype=np.int32)
    tok = np.arange(T, dtype=np.int32).reshape(NT, P).T
    return {
        "xT": c(x.reshape(T, H).T), "x_tok": c(x.reshape(T, H)),
        "W": c(np.stack([Wq, Wk, Wv, Wo], 1)),
        "rows": c(np.concatenate([bv, bo, bg, threshold.reshape(1), temperature.reshape(1)])),
        "ipack": c(np.concatenate([np.repeat(phase, 8, axis=0), bq[:, None], bk[:, None], wg.T], 1)),
        "Wgate": c(Wgate.transpose(2, 0, 1).reshape(P, NE * HID)),
        "Wup": c(Wup.transpose(2, 0, 1).reshape(P, NE * HID)),
        "Wdown": c(Wdown.transpose(2, 0, 1).reshape(4, P, NE, H).transpose(1, 2, 0, 3).reshape(P, NE * HID)),
        "c_sel": sel, "c_fill": fill,
        "cpack": c(np.concatenate([np.eye(P, dtype=f), np.triu(np.ones((P, P), f), 1), pos.reshape(P, 5 * 64),
                                   np.tile(np.arange(NE, dtype=f), (P, 1)), np.tile(np.arange(ET, dtype=f), (P, 1))],
                                  1)),
        "c_dest": c(np.stack([tok, tok + T], 1)),
    }


def kernel(**inputs):
    import concourse.bacc as bacc
    from concourse.bass_utils import run_bass_kernel_spmd

    given = {k.split("_", 2)[2]: np.asarray(v) for k, v in inputs.items()}
    arrays = launch_arrays(**given)
    nc = bacc.Bacc("TRN2", target_bir_lowering=False, num_devices=1)
    feeds, aps = {}, {}
    for name, arr in arrays.items():
        feeds[f"in_{name}"] = arr
        aps[name] = nc.dram_tensor(f"in_{name}", arr.shape, mybir.dt.from_np(arr.dtype), kind="ExternalInput").ap()
    out = nc.dram_tensor("out", (T, H), F32, kind="ExternalOutput").ap()
    build(nc, aps, out)
    r = run_bass_kernel_spmd(nc, [feeds], core_ids=[0])
    return r.results[0]["out"].reshape(B, L, H)
```

```python
import math
from contextlib import ExitStack

import numpy as np

import concourse.bass as bass
from concourse import mybir

F32 = mybir.dt.float32
BF16 = mybir.dt.bfloat16
F16 = mybir.dt.float16
I32 = mybir.dt.int32
U32 = mybir.dt.uint32
ALU = mybir.AluOpType
ACT = mybir.ActivationFunctionType
AX = mybir.AxisListType

P = 128
B, L, H = 8, 512, 128
T = B * L
NH, HD = 16, 8
NE, HID = 8, 512
NT = T // P
QB = 4
NU = NH * (B // QB)
KC = L // P
UC = QB * L
MROW = 64
NF = 5
QK_LOADS = 7 * 16
RING = 4
TW = 2 * P
ET = 2 * T // TW + NE
EB = ET * TW // P
XR = 4
AHEAD = 3
EW = (NE - 1) * HID + P
OG = 8
POOL_Q, POOL_Q_END = 396, 160
YT = 4
SX, SW = 256.0, 64.0
C_COLS = 2 * P + 5 * 64 + NE + EB
EPS = 1e-5
TPMS = 0.3
TWO_PI = 2.0 * math.pi
C1 = 6.28125
C2 = TWO_PI - C1
MAGIC = 1.5 * 2.0 ** 23


def pool_queries(g, u):
    return POOL_Q_END if isinstance(g, int) and u >= NU - 2 else POOL_Q


def wait(eng, sem, value):
    if isinstance(value, int) and value <= 0:
        return
    eng.wait_ge(sem, value)


def wait_alone(eng, turn, sem, value):
    wait(eng, sem, value)
    if not isinstance(value, int):
        eng.sem_inc(turn, 1)


def build(nc, a, out):
    ctx = ExitStack()
    with ctx:
        def sb(name, shape, dt=F32):
            return ctx.enter_context(nc.sbuf_tensor(name, shape, dt))

        def sem(name):
            return ctx.enter_context(nc.semaphore(name))

        def dram(name, shape, dt=F32):
            return nc.dram_tensor(name, shape, dt, kind="Internal").ap()

        qk_dram = dram("qk_parts", (3, 2, P, T), BF16)
        f_dram = dram("mask_key_factors", (P, NF, 64))
        g_dram = dram("mask_query_factors", (P, NF, 64))
        o_dram = dram("head_outputs", (NH, HD + 1, T))
        x1_dram = dram("first_norm", (T, H))
        y_dram = dram("expert_rows", (2 * T + ET * TW, H))

        arena = sb("arena", [P, 16384])
        probs = [arena[:, 2048 * i:2048 * (i + 1)] for i in range(KC)]
        qs = [arena[:, 8192 + 1024 * i:8192 + 1024 * (i + 1)].bitcast(BF16) for i in range(RING)]
        ks = [arena[:, 12288 + 1024 * i:12288 + 1024 * (i + 1)].bitcast(BF16) for i in range(RING)]
        qkf = [arena[:, 1024 + 1024 * i:2048 + 1024 * i].rearrange("p (s t) -> p s t", s=2) for i in range(2)]
        qkr = [arena[:, 3072 + 1024 * i:4096 + 1024 * i].rearrange("p (s t) -> p s t", s=2) for i in range(2)]
        tok_tiles = lambda ap: ap.rearrange("p (t c) -> p t c", c=H)
        x1 = tok_tiles(arena[:, 0:NT * H])
        oT = [arena[:, 4096 + 512 * i:4608 + 512 * i] for i in range(2)]
        aT = [arena[:, 5120 + 512 * i:5632 + 512 * i] for i in range(2)]
        x1T = [arena[:, 6144 + 512 * i:6656 + 512 * i] for i in range(2)]
        wpart = [[arena[:, 7168 + 2048 * (2 * w + n):7168 + 2048 * (2 * w + n + 1)].bitcast(F16) for n in range(2)]
                 for w in range(2)]
        RC = 15360
        rconst = arena[:, RC:RC + P + EB + 2 * NT + 1]
        iota_p, spare_row = rconst[:, 0:P], rconst[:, P:P + EB]
        number1 = rconst[:, P + EB:P + EB + 2 * NT]
        partition = rconst[:, P + EB + 2 * NT:]
        RC += P + EB + 2 * NT + 1
        source, result = (arena[:, RC + EB * k:RC + EB * (k + 1)] for k in range(2))
        RC += 2 * EB
        place, tile_of, gatew = (arena[:, RC + 2 * NT * k:RC + 2 * NT * (k + 1)] for k in range(3))
        pos_i, pos_m, pos_d = (arena[:, RC + 2 * NT * k:RC + 2 * NT * (k + 1)].bitcast(I32) for k in range(3, 6))
        RC += 12 * NT
        gidx, sidx = ([arena[:, RC + 8 * k + 2 * i:RC + 8 * k + 2 * i + 2].bitcast(I32) for i in range(XR)]
                      for k in range(2))

        v_all = sb("v_all", [P, NH, NT, HD + 1])
        spare = v_all[:].rearrange("p h t d -> p (h t d)")
        table = lambda k: spare[:, 256 * k:256 * (k + 1)]
        lg, mx, asg, psel = (table(k).rearrange("p (t e) -> p t e", e=NE) for k in range(4))
        oh = [table(4 + k).rearrange("p (t e) -> p t e", e=NE) for k in range(2)]
        inc, exc, posn = (table(6 + k).rearrange("p (e t) -> p e t", e=NE) for k in range(3))
        ix = table(9).bitcast(U32).rearrange("p (t e) -> p t e", e=NE)
        zer = table(10)
        cmp = spare[:, 11 * 256:11 * 256 + ET * NE].rearrange("p (t e) -> p t e", e=NE)
        xs = [[spare[:, 3400 + H * (2 * i + n):3400 + H * (2 * i + n + 1)] for n in range(2)] for i in range(XR)]
        v_cur = [sb(f"v_cur{i}", [P, NT, HD + 1]) for i in range(2)]
        mask = [sb(f"mask{i}", [P, KC, L]) for i in range(2)]
        sg = [mask[0][:, i, :] for i in range(2)]
        sel = mask[0][:, 0:2, :].rearrange("p k (b c) -> p (k b) c", c=P)
        hh = [mask[0][:, 2 + i, :] for i in range(2)]
        stats = mask[1][:, 2, 0:NT * 6].rearrange("p (t c) -> p t c", c=6)
        mv = mask[1][:, 2, NT * 6:NT * 8].rearrange("p (t c) -> p t c", c=2)
        e_buf = [sb(f"e_buf{i}", [P, 2, L]) for i in range(2)]
        l_buf = sb("l_buf", [P, 2, L])
        at_j = [arena[:, 4096 + 512 * i:4608 + 512 * i].bitcast(F16).rearrange("p (m j) -> p m j", m=OG)
                for i in range(3)]
        at_i = [arena[:, 5632 + 320 * i:5952 + 320 * i].bitcast(F16).rearrange("p (m i) -> p m i", m=OG)
                for i in range(3)]
        at_v = [part.bitcast(F16).rearrange("p (m v i) -> p m v i", m=OG, v=2)
                for part in [spare[:, 3400:4040]] + [e[:].rearrange("p i t -> p (i t)")[:, 0:640] for e in e_buf]]
        den, rden = e_buf[0][:, 0, :], e_buf[0][:, 1, :]
        l_flat = l_buf[:].rearrange("p i t -> p (i t)")
        yo = [l_flat[:, TW * i:TW * (i + 1)] for i in range(XR)]
        xT = [[e_buf[1][:, 0, P * (2 * i + n):P * (2 * i + n + 1)].bitcast(F16) for n in range(2)] for i in range(2)]
        fac = [sb(f"fac{i}", [NF, 2, 8, 64]) for i in range(2)]
        o_sb = [sb(f"o_sb{i}", [P, L]) for i in range(2)]
        xbo = sb("xbo", [P, NT, H])
        wgate = sb("wgate", [P, NE * HID])
        xb = [wgate[:, b * L:(b + 1) * L] for b in range(B)]
        wup = sb("wup", [P, NE * HID])
        wdown = sb("wdown", [P, NE * HID])
        parts = [part.bitcast(BF16).rearrange("p (n s t) -> p n s t", n=3, s=2) for part in
                 (arena[:, 5120:6656], arena[:, 6656:8192], wup[:, 0:1536], wup[:, 1536:3072])]
        z_all = tok_tiles(wgate[:])
        yg = [[tok_tiles(wup[:, YT * H * (2 * i + s):YT * H * (2 * i + s + 1)]) for s in range(2)] for i in range(4)]
        wqkvo = sb("wqkvo", [P, 4, H])
        bqs = sb("bqs", [P, 1])
        tmp1 = sb("tmp1", [P, 4])
        ang = sb("ang", [P, 3, 64])
        rnd = sb("rnd", [P, 3, 64])
        aby = sb("aby", [P, 3, 64])
        sn = sb("sn", [P, 3, 64])
        cs = sb("cs", [P, 3, 64])
        fk = sb("fk", [P, NF, 64])
        gq = sb("gq", [P, NF, 64])
        bias = sb("bias", [P, 5])
        cpack = sb("cpack", [P, C_COLS])
        ident, tri = cpack[:, 0:P], cpack[:, P:2 * P]
        pos = cpack[:, 2 * P:2 * P + 5 * 64].rearrange("p (k t) -> p k t", k=5)
        iota8, iotat = cpack[:, C_COLS - EB - NE:C_COLS - EB], cpack[:, C_COLS - EB:C_COLS]
        ipack = sb("ipack", [P, 3 + 2 + NE])
        ph, bqk, wr = ipack[:, 0:3], ipack[:, 3:5], ipack[:, 5:5 + NE]
        rows = sb("rows", [P, 2 * H + NE + 2])
        bvb, bob, bgb, tt = rows[:, 0:H], rows[:, H:2 * H], rows[:, 2 * H:2 * H + NE], rows[:, 2 * H + NE:]
        bias2 = sb("bias2", [P, 1])
        neg_max = sb("neg_max", [P, RING, 16])
        m_parts = sb("m_parts", [16, RING, 2, P], BF16)
        sd = sb("sd", [P, NT])
        rstd = sb("rstd", [P, NT])
        ixf = sb("ixf", [P, NT, 2])
        ones = sb("ones", [P, P])
        cnt = sb("cnt", [P, NE])
        cnti = sb("cnti", [P, NE], I32)
        tls = sb("tls", [P, NE])
        cumt = sb("cumt", [P, NE])
        base = sb("base", [P, NE])
        slotf = sb("slotf", [P, 2, NT])
        tef = sb("tef", [P, ET])
        te = sb("te", [P, ET], I32)
        dlt = sb("dlt", [P, NT])
        edl = sb("edl", [P, NT])
        edp = sb("edp", [P, NT])

        banks = [ctx.enter_context(nc.psum_tensor(f"bank{i}", [P, 1024], F32)) for i in range(4)]
        st = [banks[0], banks[1]]
        sm = [banks[2][:, 0:512], banks[2][:, 512:1024]]
        pv = banks[3][:, 0:512]
        misc = banks[3][:, 512:1024]

        names = """consts_loaded weights_loaded expert_w_loaded trig_ready sincos_ready
        factors_ready proj_ready v_ready evac_done v_used split_step split_done xbo_ready
        st_ready exp_done sm_ready sm_done mt_ready mt_used msub
        val_ready val_used clamp_done ln_done mask_ready
        v_cur_ready pv_step pv_evac pool_mul dve_mul pv_init x_tok_loaded p1_ready sp_turn pool_turn sel_loaded
        den_loaded rden_ready bc_ready aT_ready y_ready resid_ready stats_done mv_done sd_ready
        x1_ready x1_stored x1t_ready x1t_copied logit_ready edelta_ready rw_ready count_ready slots_ready
        tiles_ready top_ready lg_taken dlink zeroed
        route_loaded w_scaled w_split norm_ready place_ready tile_ready row_ready part_ready table_step y1_ready meta_ready
        xT_ready xhi_ready xlo_ready gu_ready silu_done h_ready down_done yo_ready
        z_ready z_stats sd2_ready out_ready stored f_stored """.split()
        S = {n: sem(n) for n in names}
        s2 = {n: [sem(f"{n}{i}") for i in range(k)] for n, k in
              (("x_loaded", B), ("parts_stored", 4), ("qk_loaded", 4), ("m_loaded", 4), ("fac_loaded", 2),
               ("o_stored", 2), ("oT_loaded", 2), ("xs_loaded", XR), ("yg_loaded", 4), ("y_scattered", XR))}

        shift = edp

        block = ctx.enter_context(nc.Block())

        def loop(eng, first, last, body, peel_last):
            body(first)
            with eng.Fori(first + 1, last - (1 if peel_last else 0)) as g:
                body(g)
            if peel_last:
                body(last - 1)

        @block.sync
        def _(sp):
            sp.dma_start(xb[0], a["xT"][:, 0:L]).then_inc(s2["x_loaded"][0], 16)
            for t, n in ((ipack, "ipack"), (cpack, "cpack")):
                sp.dma_start(t[:], a[n]).then_inc(S["consts_loaded"], 16)
            for b in range(2, B, 2):
                sp.dma_start(xb[b], a["xT"][:, b * L:(b + 1) * L]).then_inc(s2["x_loaded"][b], 16)
            sp.wait_ge(S["factors_ready"], 1)
            sp.dma_start(f_dram, fk[:]).then_inc(S["f_stored"], 16)
            sp.dma_start(g_dram, gq[:]).then_inc(S["f_stored"], 16)
            sp.wait_ge(S["f_stored"], 32)

            def load_fac(slot_, hv):
                for s, dr in ((0, f_dram), (1, g_dram)):
                    sp.dma_start(fac[slot_][:, s], dr[bass.ds(hv * 8, 8)].rearrange("c f t -> f c t")
                                 ).then_inc(s2["fac_loaded"][slot_], 16)

            def load_qk(r, head, q):
                at = 0
                for n in (3, 2, 1):
                    rows = slice(at * HD, (at + n) * HD)
                    sp.dma_start(qs[r][rows, :], qk_dram[3 - n, 0, bass.ds(head * HD, HD), q * UC:(q + 1) * UC]
                                 .unsqueeze(0).broadcast_to([n, HD, UC])).then_inc(s2["qk_loaded"][r], 16)
                    sp.dma_start(ks[r][rows, :], qk_dram[0:n, 1, bass.ds(head * HD, HD), q * UC:(q + 1) * UC]
                                 ).then_inc(s2["qk_loaded"][r], 16)
                    at += n
                sp.dma_start(qs[r][MROW:MROW + 2, :], ks[r][MROW + 2:MROW + 4, :]).then_inc(s2["qk_loaded"][r], 16)

            def store_max(r):
                for n in range(2):
                    sp.dma_start(qs[r][MROW + n:MROW + n + 1, :], m_parts[:, r, n, :]
                                 ).then_inc(s2["m_loaded"][r], 16)

            def store_o(par, head, q):
                for b in range(QB):
                    c = (q * QB + b) * L
                    sp.dma_start(o_dram[bass.ds(head, 1), :, c:c + L], o_sb[par][32 * b:32 * b + HD + 1, :]
                                 ).then_inc(s2["o_stored"][par], 16)

            def store_parts(b):
                sp.wait_ge(S["split_done"], b + 1)
                sp.dma_start(qk_dram[:, :, :, b * L:(b + 1) * L].rearrange("n s p t -> p n s t"),
                             parts[b % 4]).then_inc(s2["parts_stored"][b % 4], 16)

            load_fac(0, 0)
            load_fac(1, 1)
            sp.wait_ge(S["zeroed"], 2)
            for q in range(2):
                for b in range(4 * q, 4 * q + 4):
                    store_parts(b)
                for i in range(4):
                    sp.wait_ge(s2["parts_stored"][i], 16 * (q + 1))
                load_qk(q, 0, q)
            for q in range(2):
                load_qk(2 + q, 1, q)
            sp.wait_ge(S["mt_used"], 1)
            store_max(0)

            def attend(g):
                peeled = isinstance(g, int)
                for r in range(4):
                    u = 4 * g + r
                    lastg = peeled and g == NU // 4 - 1
                    if not (lastg and r == 3):
                        wait_alone(sp, S["sp_turn"], S["mt_used"], u + 2)
                        store_max((r + 1) % 4)
                    if peeled and g == 0:
                        if r < 3:
                            sp.dma_start(((wgate, wup, wdown)[r])[:], a[("Wgate", "Wup", "Wdown")[r]]
                                         ).then_inc(S["expert_w_loaded"], 16)
                        else:
                            sp.dma_start(xbo[:], a["x_tok"].rearrange("(t p) c -> p t c", p=P)
                                         ).then_inc(S["x_tok_loaded"], 16)
                    if not (peeled and u == 0):
                        wait_alone(sp, S["sp_turn"], S["pv_evac"], u)
                        store_o((r + 1) % 2, 2 * g + (r - 1) // 2, (r + 1) % 2)
                    hf = 2 * g + r // 2 + 2
                    if r % 2 == 0 and not (peeled and g == NU // 4 - 1):
                        wait_alone(sp, S["sp_turn"], S["val_ready"], 4 * hf - 4)
                        load_fac((r // 2) % 2, hf)
                    if not lastg:
                        wait_alone(sp, S["sp_turn"], S["st_ready"], 8 * (u + 1))
                        load_qk(r, 2 * (g + 1) + r // 2, r % 2)

            loop(sp, 0, NU // 4, attend, True)
            sp.wait_ge(S["pool_mul"], NU * KC - 2 * KC)
            sp.wait_ge(S["dve_mul"], NU * KC - 2 * KC)
            sp.dma_start(sel, a["c_sel"]).then_inc(S["sel_loaded"], 16)
            sp.wait_ge(S["pv_evac"], NU)
            store_o((NU - 1) % 2, NH - 1, 1)
            for i in range(2):
                sp.wait_ge(s2["o_stored"][i], 64 * NU // 2)
            sp.dma_start(den, o_dram[:, HD, :].rearrange("h (b t) -> h b t", b=B)).then_inc(S["den_loaded"], 16)

            def load_oT(g):
                for i in range(2):
                    wait_alone(sp, S["sp_turn"], S["aT_ready"], 2 * g + i - 1)
                    sp.dma_start(oT[i], o_dram[:, 0:HD, bass.ds((2 * g + i) * L, L)]
                                 ).then_inc(s2["oT_loaded"][i], 16)

            loop(sp, 0, 4, load_oT, False)
            sp.dma_start(rconst, a["c_route"]).then_inc(S["route_loaded"], 16)
            for b in range(0, B, 2):
                sp.wait_ge(S["x1_ready"], 4 * b + 8)
                sp.dma_start(x1_dram[b * L:(b + 2) * L, :].rearrange("(t p) c -> p t c", p=P),
                             x1[:, 4 * b:4 * b + 8, :]).then_inc(S["x1_stored"], 16)
            for r in range(XR):
                sp.wait_ge(s2["y_scattered"][r], 32 * (ET // XR))
            for k in range(NT // YT):
                wait(sp, S["z_ready"], k - 3)
                for s in range(2):
                    at = s * T + k * YT * P
                    sp.dma_start(yg[k % 4][s], y_dram[at:at + YT * P, :].rearrange("(t p) c -> p t c", p=P)
                                 ).then_inc(s2["yg_loaded"][k % 4], 16)
            for k in range(NT // YT):
                sp.wait_ge(S["out_ready"], YT * (k + 1))
                sp.dma_start(out[k * YT * P:(k + 1) * YT * P, :].rearrange("(t p) c -> p t c", p=P),
                             z_all[:, YT * k:YT * (k + 1), :]).then_inc(S["stored"], 16)
            sp.wait_ge(S["stored"], 16 * (NT // YT))

        @block.tensor
        def _(pe):
            mm = nc.tensor.matmul
            def project(b):
                i = b % 2
                pe.wait_ge(s2["x_loaded"][b], 16)
                wait(pe, S["evac_done"], b - 1)
                for s in range(2):
                    last = mm(st[i][:, s * L:(s + 1) * L], wqkvo[:, s, :], xb[b], start=True, stop=True)
                last.then_inc(S["proj_ready"], 1)
                wait(pe, S["v_used"], b - 1)
                for c in range(4):
                    last = mm(sm[i][:, c * P:(c + 1) * P], xb[b][:, c * P:(c + 1) * P], wqkvo[:, 2, :],
                              start=True, stop=True)
                last.then_inc(S["v_ready"], 1)

            def s_chunk(r, b, c, k):
                pe.wait_ge(S["sm_done"], k - 1) if not (isinstance(k, int) and k < 2) else None
                mm(sm[c % 2], qs[r][:, b * L + c * P:b * L + (c + 1) * P], ks[r][:, b * L:(b + 1) * L],
                   start=True, stop=True).then_inc(S["sm_ready"], 1)

            def turn_max(r, u):
                pe.wait_ge(S["sm_done"], 16 * (u + 1))
                nc.tensor.transpose(misc[0:16, 0:P], neg_max[:, r, :], ident).then_inc(S["mt_ready"], 1)

            def mask_arg(par, kc):
                mm(misc, fac[par][:, 0].rearrange("f c t -> f (c t)")[:, kc * P:(kc + 1) * P],
                   fac[par][:, 1].rearrange("f c t -> f (c t)"), start=True, stop=True
                   ).then_inc(S["val_ready"], 1)

            pe.wait_ge(S["weights_loaded"], 16)
            pe.wait_ge(S["pv_init"], 1)
            for b in range(B):
                project(b)
            pe.wait_ge(S["evac_done"], B)
            pe.wait_ge(S["v_used"], B)

            def first_arg(v):
                if v % 4 == 0:
                    pe.wait_ge(s2["fac_loaded"][v // 4], 32)
                wait(pe, S["val_used"], v)
                mask_arg(v // 4, v % 4)

            first_arg(0)
            first_arg(1)
            pe.wait_ge(s2["qk_loaded"][0], QK_LOADS)
            for k in range(16):
                s_chunk(0, k // 4, k % 4, k)
                if k in (2, 5, 8, 11):
                    first_arg(k // 3 + 2)
            pe.wait_ge(S["val_used"], 6)
            turn_max(0, 0)
            pe.wait_ge(s2["qk_loaded"][1], QK_LOADS)
            for k in range(16):
                s_chunk(1, k // 4, k % 4, 16 + k)

            def sums(par, kc, n, u):
                pe.wait_ge(S["pool_mul"], n + 1)
                pe.wait_ge(S["dve_mul"], n + 1)
                if kc == 0:
                    wait(pe, S["pv_evac"], u)
                hpar, q = par
                for b in range(QB):
                    last = mm(pv[32 * b:32 * b + HD + 1, :], v_cur[hpar][:, (q * QB + b) * KC + kc, :],
                              probs[kc][:, b * L:(b + 1) * L], start=(kc == 0), stop=(kc == KC - 1))
                last.then_inc(S["pv_step"], 1)

            def attend(g):
                peeled = isinstance(g, int)
                for r in range(4):
                    u = 4 * g + r
                    last_s = peeled and u >= NU - 2
                    r2 = (r + 2) % 4
                    for kc in range(KC):
                        n = 4 * u + kc
                        if kc == 0:
                            pe.wait_ge(s2["m_loaded"][r], 32 * (g + 1))
                            if not last_s:
                                pe.wait_ge(s2["qk_loaded"][r2], QK_LOADS * (g + (1 if r < 2 else 2)))
                        for half in range(2):
                            wait(pe, S["exp_done"], 2 * n + half - 1)
                            for i in range(2):
                                b = 2 * half + i
                                last = mm(st[half][:, i * L:(i + 1) * L],
                                          ks[r][:, b * L + kc * P:b * L + (kc + 1) * P],
                                          qs[r][:, b * L:(b + 1) * L], start=True, stop=True)
                            last.then_inc(S["st_ready"], 1)
                            if not last_s:
                                s_chunk(r2, kc, half, 16 * (u + 2) + 4 * kc + half)
                        if kc == 0 and not (peeled and u == NU - 1):
                            wait(pe, S["val_used"], 6 + 2 * u) if not (peeled and u > NU - 4) else None
                            turn_max((r + 1) % 4, u + 1)
                        if kc in (1, 2) and not (peeled and u + 3 >= NU):
                            if kc == 1:
                                pe.wait_ge(S["mt_used"], u + 2)
                                hv = (r + 3) // 2
                                pe.wait_ge(s2["fac_loaded"][hv % 2], 32 * (g + 1 + hv // 2))
                            else:
                                pe.wait_ge(S["val_used"], 6 + 2 * u + 1)
                            mask_arg(((r + 3) // 2) % 2, 2 * ((r + 3) % 2) + kc - 1)
                        if not last_s:
                            s_chunk(r2, kc, 2, 16 * (u + 2) + 4 * kc + 2)
                        if not (peeled and n < 2):
                            pn = (kc + 2) % 4
                            pr = r if kc >= 2 else r - 1
                            if pn == 0 and pr % 2 == 0:
                                pe.wait_ge(S["v_cur_ready"], 2 * g + (pr // 2) + 1)
                            sums((((pr // 2) % 2), pr % 2), pn, n - 2, 4 * g + pr)
                        if not last_s:
                            s_chunk(r2, kc, 3, 16 * (u + 2) + 4 * kc + 3)

            loop(pe, 0, NU // 4, attend, True)
            for n in (NU * KC - 2, NU * KC - 1):
                sums((1, 1), n % 4, n, NU - 1)

            pe.wait_ge(S["consts_loaded"], 48)
            pe.wait_ge(S["rden_ready"], 1)
            pe.wait_ge(S["sel_loaded"], 16)

            def spread(b):
                wait(pe, S["aT_ready"], b - 1)
                mm(st[b % 2][:, 0:L], sel[:, b, :], rden, start=True, stop=True).then_inc(S["bc_ready"], 1)

            def turn_x1(b):
                pe.wait_ge(S["x1_ready"], 4 * (b + 1))
                wait(pe, S["x1t_copied"], b - 1)
                for c in range(4):
                    last = nc.tensor.transpose(sm[b % 2][:, c * P:(c + 1) * P], x1[:, 4 * b + c, :], ident)
                last.then_inc(S["x1t_ready"], 1)

            def turn_two(k):
                turn_x1(2 * k)
                turn_x1(2 * k + 1)

            def logits(k):
                wait(pe, S["lg_taken"], k - 1)
                for b in (2 * k, 2 * k + 1):
                    pe.wait_ge(S["x1t_copied"], b + 1)
                    for t in range(4 * b, 4 * b + 4):
                        last = mm((pv, misc)[k % 2][:, t * NE:(t + 1) * NE], x1T[b % 2][:, (t % 4) * P:(t % 4 + 1) * P], wr,
                                  start=True, stop=True)
                last.then_inc(S["logit_ready"], 1)

            spread(0)
            for b in range(B):
                i = b % 2
                if b + 1 < B:
                    spread(b + 1)
                pe.wait_ge(S["aT_ready"], b + 1)
                wait(pe, S["resid_ready"], b - 1)
                for c in range(4):
                    last = mm(st[i][:, L + c * P:L + (c + 1) * P], aT[i][:, c * P:(c + 1) * P], wqkvo[:, 3, :],
                              start=True, stop=True)
                last.then_inc(S["y_ready"], 1)
                if b in (4, 6):
                    turn_two(b // 2 - 2)
                if b in (5, 7):
                    logits((b - 5) // 2)
            for k in (2, 3):
                turn_two(k)
                logits(k)
            pe.wait_ge(S["count_ready"], 1)
            av = asg.rearrange("p t e -> p e t")
            mm(misc[:, 0:256], tri, av, start=True, stop=True)
            mm(misc[:, 256:512], ones[:], av, start=True, stop=True).then_inc(S["slots_ready"], 1)

            for k in range(2 * NT // OG):
                pe.wait_ge(S["place_ready"], k + 1)
                pe.wait_ge(S["row_ready"], k + 1)
                pe.wait_ge(S["part_ready"], k + 1)
                for m in range(OG):
                    last = mm(sm[1][:, 0:2 * EB], at_j[k % 3][:, m, :], at_v[k % 3][:, m].rearrange("p v i -> p (v i)"),
                              start=(k + m == 0), stop=(k * OG + m == 2 * NT - 1))
                last.then_inc(S["table_step"], 1)

            xtp, yp = banks[2], banks[3]
            pe.wait_ge(S["tiles_ready"], 1)
            pe.wait_ge(S["w_split"], 2)

            def turn_x(r, i, g):
                pe.wait_ge(s2["xs_loaded"][r], 32 * (g + 1))
                wait(pe, S["xlo_ready"], i)
                for n in range(2):
                    last = nc.tensor.transpose(xtp[:, n * P:(n + 1) * P], xs[r][n], ident)
                last.then_inc(S["xT_ready"], 1)

            def expert_of(i):
                return pe.value_load(te[0:1, bass.ds(i, 1)], min_val=0, max_val=(NE - 1) * HID)

            def gate_up(r, h, i, e):
                if h == 0:
                    pe.wait_ge(S["xlo_ready"], i + 1)
                wait(pe, S["h_ready"], 2 * i + h - 1)
                for w in range(2):
                    for c in range(2):
                        at = (2 * h + c) * P
                        for k, (n, m) in enumerate(((0, 0), (0, 1), (1, 0))):
                            last = mm(banks[h][:, 512 * w + c * TW:512 * w + (c + 1) * TW],
                                      wpart[w][n][:, at:at + EW][:, bass.ds(e, P)], xT[r % 2][m],
                                      start=(k == 0), stop=(k == 2))
                last.then_inc(S["gu_ready"], 1)

            def down(h, i, e):
                pe.wait_ge(S["h_ready"], 2 * i + h + 1)
                if h == 0:
                    wait(pe, S["yo_ready"], i)
                for c in range(2):
                    at = (2 * h + c) * P
                    for n in range(2):
                        last = mm(yp[:, 512 * n:512 * n + H], hh[h][:, c * TW + n * P:c * TW + (n + 1) * P],
                                  wdown[:, at:at + EW][:, bass.ds(e, P)], start=(2 * h + c == 0), stop=(2 * h + c == 3))
                last.then_inc(S["down_done"], 1)

            turn_x(0, 0, 0)

            def expert(g):
                peeled = isinstance(g, int)
                e = None
                for r in range(XR):
                    i = XR * g + r
                    if not (peeled and i + 1 >= ET):
                        turn_x((r + 1) % XR, i + 1, g + (1 if r == XR - 1 else 0))
                    e_old = e if r else (expert_of(i - 1) if not (peeled and i < 1) else None)
                    e = expert_of(i)
                    gate_up(r, 0, i, e)
                    if not (peeled and i < 1):
                        down(1, i - 1, e_old)
                    gate_up(r, 1, i, e)
                    down(0, i, e)

            loop(pe, 0, ET // XR, expert, True)
            down(1, ET - 1, expert_of(ET - 1))

        @block.scalar
        def _(act):
            A = nc.scalar.activation
            RS = 1.0 / math.sqrt(HD)
            for t, src, m in ((wqkvo, "W", "weights_loaded"), (rows, "rows", "consts_loaded")):
                src = a[src] if src == "W" else a[src].partition_broadcast(P)
                act.dma_start(t[:], src).then_inc(S[m], 16)
            for b in range(1, B, 2):
                act.dma_start(xb[b], a["xT"][:, b * L:(b + 1) * L]).then_inc(s2["x_loaded"][b], 16)
            act.wait_ge(S["trig_ready"], 1)
            A(sn[:], ang[:], ACT.Sin)
            A(cs[:], aby[:], ACT.Sin, bias=bias[:, 0:1], scale=-1.0).then_inc(S["sincos_ready"], 1)
            nc.scalar.preload_act_table_set("natural_log_exp_and_others")

            def project(b):
                i = b % 2
                act.wait_ge(S["proj_ready"], b + 1)
                wait(act, s2["parts_stored"][b % 4], 16 * (b // 4))
                wait(act, S["split_step"], b - 1)
                A(qkf[i][:, 0, :], st[i][:, 0:L], ACT.Identity, bias=bqs[:], scale=RS)
                A(parts[b % 4][:, 0, 0, :], st[i][:, 0:L], ACT.Identity, bias=bqs[:], scale=RS)
                A(qkf[i][:, 1, :], st[i][:, L:2 * L], ACT.Identity, bias=bqk[:, 1:2])
                A(parts[b % 4][:, 0, 1, :], st[i][:, L:2 * L], ACT.Identity, bias=bqk[:, 1:2]
                  ).then_inc(S["evac_done"], 1)

            def mask_exp(v, par, i):
                act.wait_ge(S["val_ready"], v + 1)
                A(e_buf[par][:, i, :], misc, ACT.Exp, bias=bias[:, 3:4], scale=bias[:, 2:3]
                  ).then_inc(S["val_used"], 1)

            def mask_step(w, par, k):
                if k == 0:
                    act.wait_ge(S["clamp_done"], w + 1)
                else:
                    act.wait_ge(S["ln_done"], 3 * w + k)
                func, bias_, scale = ((ACT.Ln, bias[:, 1:2], 1.0), (ACT.Exp, 0.0, -1.0), (ACT.Ln, bias[:, 4:5], 1.0))[k]
                A(e_buf[par][:], e_buf[par][:], func, bias=bias_, scale=scale).then_inc(S["ln_done"], 1)

            def mask_fin(w, par, hpar, pair):
                act.wait_ge(S["ln_done"], 3 * w + 3)
                A(mask[hpar][:, 2 * pair:2 * pair + 2, :], e_buf[par][:], ACT.Exp, scale=TPMS
                  ).then_inc(S["mask_ready"], 1)

            def take_v(head, par):
                nc.scalar.copy(v_cur[par][:], v_all[:, head]).then_inc(S["v_cur_ready"], 1)

            for b in range(B):
                project(b)
            for v in range(4):
                mask_exp(v, v // 2, v % 2)
            for w in range(2):
                for k in range(3):
                    mask_step(w, w, k)
                mask_fin(w, w, 0, w)
                if w == 0:
                    act.wait_ge(S["mask_ready"], 1)
                    mask_exp(4, 0, 0)
                    mask_exp(5, 0, 1)
            act.wait_ge(S["v_used"], B)
            nc.scalar.copy(v_cur[0][:], v_all[:, 0]).then_inc(S["v_cur_ready"], 1)
            act.wait_ge(S["split_done"], B)
            for i in range(4):
                act.wait_ge(s2["parts_stored"][i], 16 * 2)

            def attend(g):
                peeled = isinstance(g, int)
                for r in range(4):
                    u = 4 * g + r
                    fill = not (peeled and u + 2 >= NU)
                    for kc in range(KC):
                        n = 4 * u + kc
                        wait(act, S["pv_step"], n - 3)
                        for half in range(2):
                            act.wait_ge(S["st_ready"], 2 * n + half + 1)
                            A(probs[kc][:, half * 1024:(half + 1) * 1024], st[half][:], ACT.Exp
                              ).then_inc(S["exp_done"], 1)
                            if kc == 2 and half == 0 and not (peeled and u == 0):
                                copy_sums(u - 1, (r + 1) % 2, g, r)
                            if kc == 0 and fill:
                                mask_step(u + 2, r % 2, half)
                            if kc == 1 and half == 0 and fill:
                                mask_step(u + 2, r % 2, 2)
                        if kc in (1, 2) and not (peeled and u + 3 >= NU):
                            mask_exp(6 + 2 * u + kc - 1, (r + 1) % 2, kc - 1)
                        if kc == 3 and fill:
                            hv = (r + 2) // 2
                            wait(act, S["pool_mul"], 8 * (2 * g + hv - 1))
                            wait(act, S["dve_mul"], 8 * (2 * g + hv - 1))
                            mask_fin(u + 2, r % 2, hv % 2, r % 2)
                        if kc == 3 and r % 2 and not (peeled and u == NU - 1):
                            wait(act, S["pv_step"], 8 * (2 * g + r // 2))
                            take_v(2 * g + r // 2 + 1, (r // 2 + 1) % 2)

            def copy_sums(u, par, g, r):
                act.wait_ge(S["pv_step"], 4 * (u + 1))
                wait(act, s2["o_stored"][par], 64 * (2 * g + (0 if r == 0 else (r - 1) // 2)) if r else 64 * (2 * g - 1))
                nc.scalar.copy(o_sb[par][:], pv).then_inc(S["pv_evac"], 1)

            loop(act, 0, NU // 4, attend, True)
            act.wait_ge(S["pv_step"], NU * KC)
            act.wait_ge(s2["o_stored"][1], 64 * (NU // 2 - 1))
            nc.scalar.copy(o_sb[1][:], pv).then_inc(S["pv_evac"], 1)

            act.wait_ge(S["expert_w_loaded"], 48)
            for w, wt in enumerate((wgate, wup)):
                nc.scalar.mul(wpart[w][0], wt[:], SW)
                nc.scalar.mul(wt[:], wt[:], SW).then_inc(S["w_scaled"], 1)
            for k in range(4):
                tiles = slice(8 * k, 8 * k + 8)
                act.wait_ge(S["mv_done"], k + 1)
                A(sd[:, tiles], mv[:, tiles, 1], ACT.Sqrt, bias=bias2[:]).then_inc(S["sd_ready"], 1)
                act.wait_ge(S["norm_ready"], k + 1)
                for t in range(8 * k, 8 * k + 8):
                    A(x1[:, t, :], x1[:, t, :], ACT.Identity, bias=shift[:, t:t + 1], scale=rstd[:, t:t + 1]
                      ).then_inc(S["x1_ready"], 1)
                for b in (2 * k, 2 * k + 1):
                    act.wait_ge(S["x1t_ready"], b + 1)
                    nc.scalar.copy(x1T[b % 2], sm[b % 2]).then_inc(S["x1t_copied"], 1)
            act.wait_ge(S["rw_ready"], 1)
            A(edl[:], dlt[:], ACT.Exp).then_inc(S["edelta_ready"], 1)

            act.wait_ge(S["route_loaded"], 16)
            for k in range(2 * NT // OG):
                act.wait_ge(S["tile_ready"], k + 1)
                A(at_v[k % 3][:, :, 1, :], at_i[k % 3], ACT.Copy, scale=partition).then_inc(S["part_ready"], 1)

            yp = banks[3]

            def x_high(r, i):
                act.wait_ge(S["xT_ready"], i + 1)
                wait(act, S["gu_ready"], 2 * i - 2)
                nc.scalar.mul(xT[r % 2][0], banks[2][:, 0:TW], SX).then_inc(S["xhi_ready"], 1)

            def y_copy(r, i):
                act.wait_ge(S["down_done"], 2 * i + 2)
                nc.scalar.copy(yo[r].rearrange("p (n c) -> p n c", n=2),
                               yp[:].rearrange("p (n c) -> p n c", n=2)[:, :, 0:H]).then_inc(S["yo_ready"], 1)

            x_high(0, 0)

            def silu(h, i):
                act.wait_ge(S["gu_ready"], 2 * i + h + 1)
                wait(act, S["h_ready"], 2 * i + h - 1)
                A(sg[h], banks[h][:, 0:512], ACT.Silu, scale=1.0 / (SX * SW)).then_inc(S["silu_done"], 1)

            def expert(g):
                peeled = isinstance(g, int)
                for r in range(XR):
                    i = XR * g + r
                    if not (peeled and i + 1 >= ET):
                        x_high((r + 1) % XR, i + 1)
                    silu(0, i)
                    if not (peeled and i < 1):
                        y_copy((r - 1) % XR, i - 1)
                    silu(1, i)

            loop(act, 0, ET // XR, expert, True)
            y_copy(XR - 1, ET - 1)
            for k in range(NT // YT):
                tiles = slice(YT * k, YT * (k + 1))
                act.wait_ge(S["z_stats"], k + 1)
                A(sd[:, tiles], mv[:, tiles, 1], ACT.Sqrt, bias=bias2[:]).then_inc(S["sd2_ready"], 1)
                act.wait_ge(S["norm_ready"], 4 + k + 1)
                for t in range(YT * k, YT * (k + 1)):
                    A(z_all[:, t, :], z_all[:, t, :], ACT.Identity, bias=shift[:, t:t + 1], scale=rstd[:, t:t + 1]
                      ).then_inc(S["out_ready"], 1)

        @block.gpsimd
        def _(pool):
            for i in range(RING):
                nc.gpsimd.memset(arena[:, 8192 + 1024 * i:8192 + 1024 * (i + 1)], 0.0)
                last = nc.gpsimd.memset(arena[:, 12288 + 1024 * i:12288 + 1024 * (i + 1)], 0.0)
            last.then_inc(S["zeroed"], 1)
            pool.wait_ge(S["zeroed"], 1)
            for i in range(RING):
                last = nc.gpsimd.memset(ks[i][MROW:MROW + 2, :], 1.0)
            last.then_inc(S["zeroed"], 1)
            pool.wait_ge(S["zeroed"], 2)
            pool.wait_ge(S["consts_loaded"], 48)
            for b in range(B):
                pool.wait_ge(S["p1_ready"], b + 1)
                nc.gpsimd.tensor_tensor(parts[b % 4][:, 2], qkr[b % 2], parts[b % 4][:, 1], ALU.subtract
                                        ).then_inc(S["split_done"], 1)

            def attend(g):
                for r in range(4):
                    q1 = pool_queries(g, 4 * g + r)
                    for kc in range(KC):
                        n = 4 * (4 * g + r) + kc
                        pool.wait_ge(S["exp_done"], 2 * n + 2)
                        pool.wait_ge(S["mask_ready"], 2 * (2 * g + r // 2) + kc // 2 + 1)
                        pb = probs[kc].rearrange("p (b t) -> p b t", b=QB)[:, :, 0:q1]
                        nc.gpsimd.tensor_tensor(
                            pb, pb, mask[r // 2][:, kc, 0:q1].unsqueeze(1).broadcast_to([P, QB, q1]), ALU.mult
                        ).then_inc(S["pool_mul"], 1)

            loop(pool, 0, NU // 4, attend, True)
            pool.wait_ge(S["x_tok_loaded"], 16)
            for b in range(B):
                xbb = xbo[:, 4 * b:4 * b + 4, :]
                nc.gpsimd.tensor_tensor(xbb, xbb, bob.unsqueeze(1).broadcast_to([P, 4, H]), ALU.add
                                        ).then_inc(S["xbo_ready"], 1)
            for w, wt in enumerate((wgate, wup)):
                pool.wait_ge(S["w_scaled"], w + 1)
                nc.gpsimd.tensor_tensor(wpart[w][1], wt[:], wpart[w][0], ALU.subtract).then_inc(S["w_split"], 1)

            def gather(r, i):
                wait_alone(pool, S["pool_turn"], S["meta_ready"], i + 1)
                wait_alone(pool, S["pool_turn"], S["xT_ready"], i - XR + 1)
                nc.gpsimd.indirect_dma_start(
                    xs[r], None, x1_dram, bass.IndirectOffsetOnAxis(ap=idx[r][:, 0:1].bitcast(U32), axis=0)
                ).then_inc(s2["xs_loaded"][r], 16)

            pool.wait_ge(S["route_loaded"], 16)
            for k in range(2 * NT // OG):
                pool.wait_ge(S["tile_ready"], k + 1)
                nc.gpsimd.tensor_tensor(
                    at_v[k % 3][:, :, 0, :], at_i[k % 3],
                    number1[:, OG * k:OG * (k + 1)].unsqueeze(2).broadcast_to([P, OG, EB]), ALU.mult
                ).then_inc(S["row_ready"], 1)

            def gather(r, i):
                wait_alone(pool, S["pool_turn"], S["meta_ready"], i + 1)
                wait_alone(pool, S["pool_turn"], S["xT_ready"], i - XR + 1)
                for n in range(2):
                    nc.gpsimd.indirect_dma_start(
                        xs[r][n], None, x1_dram,
                        bass.IndirectOffsetOnAxis(ap=gidx[r][:, n:n + 1].bitcast(U32), axis=0)
                    ).then_inc(s2["xs_loaded"][r], 16)

            pool.wait_ge(S["x1_stored"], 16 * B // 2)
            for i in range(AHEAD):
                gather(i, i)

            def expert(g):
                peeled = isinstance(g, int)
                for r in range(XR):
                    i = XR * g + r
                    if not (peeled and i + AHEAD >= ET):
                        gather((r + AHEAD) % XR, i + AHEAD)
                    wait_alone(pool, S["pool_turn"], S["yo_ready"], i + 1)
                    for n in range(2):
                        nc.gpsimd.indirect_dma_start(
                            y_dram, bass.IndirectOffsetOnAxis(ap=sidx[r][:, n:n + 1].bitcast(U32), axis=0),
                            yo[r][:, n * H:(n + 1) * H], None).then_inc(s2["y_scattered"][r], 16)

            loop(pool, 0, ET // XR, expert, True)
            for k in range(NT // YT):
                pool.wait_ge(s2["yg_loaded"][k % 4], 32 * (k // 4 + 1))
                nc.gpsimd.tensor_tensor(
                    yg[k % 4][1], yg[k % 4][1],
                    gatew[:, NT + YT * k:NT + YT * (k + 1)].unsqueeze(2).broadcast_to([P, YT, H]), ALU.mult
                ).then_inc(S["y1_ready"], 1)
                pool.wait_ge(S["y1_ready"], 2 * k + 1)
                nc.gpsimd.tensor_tensor(yg[k % 4][1], yg[k % 4][1], x1[:, YT * k:YT * (k + 1), :], ALU.add
                                        ).then_inc(S["y1_ready"], 1)

        @block.vector
        def _(dve):
            V = nc.vector
            chain = [0]

            def link(ins):
                chain[0] += 1
                ins.then_inc(S["dlink"], 1)
                dve.wait_ge(S["dlink"], chain[0])

            V.memset(bias[:, 0:1], math.pi / 2)
            V.memset(bias[:, 1:2], 1.0)
            V.memset(bias[:, 4:5], 1e-6)
            V.memset(bias2[:], EPS)
            V.memset(ones[:], 1.0)
            V.memset(v_all[:, :, :, HD], 1.0)
            V.memset(pv, 0.0).then_inc(S["pv_init"], 1)
            dve.wait_ge(S["consts_loaded"], 48)
            link(V.tensor_scalar(tmp1[:, 0:1], tt[:, 1:2], 1e-6, None, ALU.add))
            link(V.reciprocal(tmp1[:, 1:2], tmp1[:, 0:1]))
            V.tensor_scalar(bias[:, 2:3], tmp1[:, 1:2], -1.0, None, ALU.mult)
            V.tensor_tensor(bias[:, 3:4], tmp1[:, 1:2], tt[:, 0:1], ALU.mult)
            link(V.tensor_scalar(bqs[:], bqk[:, 0:1], 1.0 / math.sqrt(HD), None, ALU.mult))
            for i in range(3):
                last = V.tensor_scalar(ang[:, i, :], pos[:, i, :], ph[:, i:i + 1], None, ALU.add)
            link(last)
            link(V.tensor_scalar(rnd[:], ang[:], 1.0 / TWO_PI, MAGIC, ALU.mult, ALU.add))
            link(V.tensor_scalar(rnd[:], rnd[:], -MAGIC, None, ALU.add))
            link(V.scalar_tensor_tensor(ang[:], rnd[:], -C1, ang[:], ALU.mult, ALU.add))
            link(V.scalar_tensor_tensor(ang[:], rnd[:], -C2, ang[:], ALU.mult, ALU.add))
            link(V.tensor_scalar(ang[:], ang[:], 3.1415925, -3.1415925, ALU.min, ALU.max))
            link(V.tensor_scalar(aby[:], ang[:], -1.0, None, ALU.mult))
            link(V.tensor_tensor(aby[:], aby[:], ang[:], ALU.max))
            V.tensor_copy(tmp1[:, 2:3], tmp1[:, 1:2]).then_inc(S["trig_ready"], 1)
            dve.wait_ge(S["sincos_ready"], 1)
            cb, sbb = pos[:, 3, :], pos[:, 4, :]
            V.tensor_copy(fk[:, 0, :], cs[:, 1, :])
            V.tensor_copy(gq[:, 0, :], sn[:, 0, :])
            V.tensor_tensor(fk[:, 1, :], sn[:, 1, :], cb, ALU.mult)
            V.tensor_copy(gq[:, 1, :], cs[:, 2, :])
            V.scalar_tensor_tensor(fk[:, 2, :], sn[:, 1, :], -1.0, sbb, ALU.mult, ALU.mult)
            V.tensor_copy(gq[:, 2, :], sn[:, 2, :])
            V.tensor_copy(fk[:, 3, :], cb)
            V.tensor_tensor(gq[:, 3, :], sn[:, 2, :], cs[:, 0, :], ALU.mult)
            V.tensor_copy(fk[:, 4, :], sbb)
            V.tensor_tensor(gq[:, 4, :], cs[:, 2, :], cs[:, 0, :], ALU.mult).then_inc(S["factors_ready"], 1)

            def project(b):
                i = b % 2
                dve.wait_ge(S["v_ready"], b + 1)
                V.tensor_tensor(
                    v_all[:, :, 4 * b:4 * b + 4, 0:HD].rearrange("p h c d -> p c h d"),
                    sm[i].rearrange("p (c h d) -> p c h d", c=4, h=NH),
                    bvb.rearrange("p (h d) -> p h d", h=NH).unsqueeze(1).broadcast_to([P, 4, NH, HD]),
                    ALU.add).then_inc(S["v_used"], 1)
                dve.wait_ge(S["evac_done"], b + 1)
                wait(dve, S["split_done"], b - 1)
                V.tensor_tensor(qkr[i], qkf[i], parts[b % 4][:, 0], ALU.subtract).then_inc(S["split_step"], 1)
                dve.wait_ge(S["split_step"], b + 1)
                V.tensor_copy(parts[b % 4][:, 1], qkr[i]).then_inc(S["p1_ready"], 1)

            def row_max(r, c16, k):
                dve.wait_ge(S["sm_ready"], k + 1)
                V.tensor_reduce(neg_max[:, r, c16:c16 + 1], sm[c16 % 2], AX.X, ALU.max, negate=True
                                ).then_inc(S["sm_done"], 1)

            def split_max(r, u):
                dve.wait_ge(S["mt_ready"], u + 1)
                V.tensor_copy(m_parts[:, r, 0, :], misc[0:16, 0:P]).then_inc(S["msub"], 1)
                dve.wait_ge(S["msub"], u + 1)
                V.tensor_tensor(m_parts[:, r, 1, :], misc[0:16, 0:P], m_parts[:, r, 0, :], ALU.subtract
                                ).then_inc(S["mt_used"], 1)

            def clamp(w, par):
                dve.wait_ge(S["val_used"], 2 * w + 2)
                V.tensor_scalar(e_buf[par][:], e_buf[par][:], 1e18, None, ALU.min).then_inc(S["clamp_done"], 1)

            for b in range(B):
                project(b)
            for k in range(16):
                row_max(0, k, k)
                if k in (5, 9):
                    clamp(k // 4 - 1, k // 4 - 1)
            split_max(0, 0)
            for k in range(16, 32):
                row_max(1, k % 16, k)
                if k == 17:
                    clamp(2, 0)

            def apply_mask(kc, n, hpar, mr, q0):
                dve.wait_ge(S["exp_done"], 2 * n + 2)
                dve.wait_ge(S["mask_ready"], mr)
                pb = probs[kc].rearrange("p (b t) -> p b t", b=QB)[:, :, q0:]
                V.tensor_tensor(pb, pb, mask[hpar][:, kc, q0:].unsqueeze(1).broadcast_to([P, QB, L - q0]), ALU.mult
                                ).then_inc(S["dve_mul"], 1)

            def attend(g):
                peeled = isinstance(g, int)
                for r in range(4):
                    u = 4 * g + r
                    for kc in range(KC):
                        n = 4 * u + kc
                        if not (peeled and u >= NU - 2):
                            for c in range(2):
                                row_max((r + 2) % 4, 4 * kc + c, 16 * (u + 2) + 4 * kc + c)
                        if kc == 0 and not (peeled and u == NU - 1):
                            split_max((r + 1) % 4, u + 1)
                        if not (peeled and n == 0):
                            pr = r if kc else r - 1
                            apply_mask((kc + 3) % 4, n - 1, (pr // 2) % 2,
                                       2 * (2 * g + pr // 2) + ((kc + 3) % 4) // 2 + 1, pool_queries(g, 4 * g + pr))
                        if not (peeled and u >= NU - 2):
                            for c in range(2, 4):
                                row_max((r + 2) % 4, 4 * kc + c, 16 * (u + 2) + 4 * kc + c)
                        if kc == 3 and not (peeled and u + 3 >= NU):
                            clamp(u + 3, (r + 1) % 2)

            loop(dve, 0, NU // 4, attend, True)
            apply_mask(3, NU * KC - 1, 1, 2 * NH, pool_queries(NU // 4 - 1, NU - 1))

            def residual(b):
                dve.wait_ge(S["y_ready"], b + 1)
                dve.wait_ge(S["xbo_ready"], b + 1)
                V.tensor_tensor(x1[:, 4 * b:4 * b + 4, :], st[b % 2][:, L:2 * L].rearrange("p (c d) -> p c d", c=4),
                                xbo[:, 4 * b:4 * b + 4, :], ALU.add).then_inc(S["resid_ready"], 1)
                dve.wait_ge(S["resid_ready"], b + 1)
                for t in range(4 * b, 4 * b + 4):
                    V.bn_stats(stats[:, t, :], x1[:, t, :]).then_inc(S["stats_done"], 1)

            def moments(k, n, ready):
                for t in range(n * k, n * (k + 1)):
                    last = V.bn_aggr(mv[:, t, :], stats[:, t, :])
                last.then_inc(S[ready], 1)

            def norm(k, n, ready):
                tiles = slice(n * k, n * (k + 1))
                dve.wait_ge(S[ready], k + 1)
                link(V.reciprocal(rstd[:, tiles], sd[:, tiles]))
                V.scalar_tensor_tensor(shift[:, tiles], mv[:, tiles, 0], -1.0, rstd[:, tiles], ALU.mult, ALU.mult
                                       ).then_inc(S["norm_ready"], 1)

            def top2(k):
                tiles = slice(8 * k, 8 * k + 8)
                dve.wait_ge(S["logit_ready"], k + 1)
                V.tensor_tensor(lg[:, tiles], (pv, misc)[k % 2][:, 64 * k:64 * (k + 1)].rearrange(
                    "p (t e) -> p t e", e=NE), bgb.unsqueeze(1).broadcast_to([P, 8, NE]), ALU.add
                    ).then_inc(S["lg_taken"], 1)
                dve.wait_ge(S["lg_taken"], k + 1)
                for t in range(8 * k, 8 * k + 8):
                    last = V.max(mx[:, t, :], lg[:, t, :])
                link(last)
                for t in range(8 * k, 8 * k + 8):
                    last = V.max_index(ix[:, t, :], mx[:, t, :], lg[:, t, :])
                last.then_inc(S["top_ready"], 1)

            dve.wait_ge(S["den_loaded"], 16)
            V.reciprocal(rden, den).then_inc(S["rden_ready"], 1)
            for b in range(B):
                i = b % 2
                dve.wait_ge(s2["oT_loaded"][i], 16 * (b // 2 + 1))
                dve.wait_ge(S["bc_ready"], b + 1)
                wait(dve, S["y_ready"], b - 1)
                V.tensor_tensor(aT[i], st[i][:, 0:L], oT[i], ALU.mult).then_inc(S["aT_ready"], 1)
                if b:
                    residual(b - 1)
                if b in (2, 4, 6):
                    dve.wait_ge(S["stats_done"], 4 * b)
                    moments(b // 2 - 1, 8, "mv_done")
                if b in (3, 5, 7):
                    norm((b - 3) // 2, 8, "sd_ready")
            residual(B - 1)
            dve.wait_ge(S["stats_done"], NT)
            moments(3, 8, "mv_done")
            link(V.memset(zer, 0.0))
            top2(0)
            norm(3, 8, "sd_ready")
            for k in range(1, 4):
                top2(k)
            dve.wait_ge(S["top_ready"], 4)
            V.tensor_tensor(dlt[:], mx[:, :, 1], mx[:, :, 0], ALU.subtract).then_inc(S["rw_ready"], 1)
            link(V.tensor_copy(ixf[:], ix[:, :, 0:2]))
            for s in range(2):
                last = V.tensor_tensor(oh[s], iota8.unsqueeze(1).broadcast_to([P, NT, NE]),
                                       ixf[:, :, s].unsqueeze(2).broadcast_to([P, NT, NE]), ALU.is_equal)
            link(last)
            V.tensor_tensor(asg, oh[0], oh[1], ALU.add).then_inc(S["count_ready"], 1)
            dve.wait_ge(S["slots_ready"], 1)
            before = misc[:, 0:256].rearrange("p (e t) -> p e t", e=NE)
            total = misc[:, 256:512]
            link(V.tensor_tensor_scan(inc.rearrange("p e t -> p (e t)"), zer, total, 0.0, ALU.add, ALU.add))
            link(V.tensor_tensor(exc.rearrange("p e t -> p (e t)"), inc.rearrange("p e t -> p (e t)"), total,
                                 ALU.subtract))
            link(V.tensor_tensor(cnt[:], inc[:, :, NT - 1], exc[:, :, 0], ALU.subtract))
            link(V.tensor_scalar(cnti[:], cnt[:], float(TW - 1), None, ALU.add))
            link(V.tensor_scalar(cnti[:], cnti[:], 8, None, ALU.arith_shift_right))
            link(V.tensor_copy(tls[:], cnti[:]))
            link(V.tensor_tensor_scan(cumt[:], zer[:, 0:NE], tls[:], 0.0, ALU.add, ALU.add))
            link(V.tensor_tensor(base[:], cumt[:], tls[:], ALU.subtract))
            link(V.scalar_tensor_tensor(base[:], base[:], float(TW), exc[:, :, 0], ALU.mult, ALU.subtract))
            link(V.tensor_tensor(posn, before, exc, ALU.add))
            link(V.tensor_tensor(posn, posn, base[:].unsqueeze(2).broadcast_to([P, NE, NT]), ALU.add))
            for s in range(2):
                link(V.tensor_tensor(psel, oh[s], posn.rearrange("p e t -> p t e"), ALU.mult))
                link(V.tensor_reduce(slotf[:, s, :], psel, AX.X, ALU.add))
            dve.wait_ge(S["edelta_ready"], 1)
            link(V.tensor_scalar(edp[:], edl[:], 1.0, None, ALU.add))
            link(V.reciprocal(gatew[:, 0:NT], edp[:]))
            V.tensor_tensor(gatew[:, NT:2 * NT], gatew[:, 0:NT], edl[:], ALU.mult)
            link(V.tensor_copy(pos_i, slotf[:].rearrange("p s t -> p (s t)")))
            V.tensor_scalar(pos_m, pos_i, P - 1, None, ALU.bitwise_and)
            link(V.tensor_scalar(pos_d, pos_i, 7, None, ALU.arith_shift_right))
            V.tensor_copy(place, pos_m)
            link(V.tensor_copy(tile_of, pos_d))
            dve.wait_ge(S["route_loaded"], 16)
            for k in range(2 * NT // OG):
                wait(dve, S["table_step"], k - 2)
                ms = slice(OG * k, OG * (k + 1))
                V.tensor_tensor(at_i[k % 3], iotat.unsqueeze(1).broadcast_to([P, OG, EB]),
                                tile_of[:, ms].unsqueeze(2).broadcast_to([P, OG, EB]), ALU.is_equal
                                ).then_inc(S["tile_ready"], 1)
                V.tensor_tensor(at_j[k % 3], iota_p.unsqueeze(1).broadcast_to([P, OG, P]),
                                place[:, ms].unsqueeze(2).broadcast_to([P, OG, P]), ALU.is_equal
                                ).then_inc(S["place_ready"], 1)
            link(V.tensor_tensor(cmp, iotat[:, 0:ET].unsqueeze(2).broadcast_to([P, ET, NE]),
                                 cumt[:].unsqueeze(1).broadcast_to([P, ET, NE]), ALU.is_ge))
            link(V.tensor_reduce(tef[:], cmp, AX.X, ALU.add))
            link(V.tensor_scalar(tef[:], tef[:], float(NE - 1), float(HID), ALU.min, ALU.mult))
            V.tensor_copy(te[:], tef[:]).then_inc(S["tiles_ready"], 1)
            dve.wait_ge(S["table_step"], 2 * NT // OG)
            link(V.tensor_copy(result, sm[1][:, EB:2 * EB]))
            link(V.scalar_tensor_tensor(result, sm[1][:, 0:EB], float(P), result, ALU.mult, ALU.add))
            link(V.tensor_scalar(source, result, float(T + P) - 0.5, float(-T), ALU.is_ge, ALU.mult))
            link(V.tensor_tensor(source, source, result, ALU.add))
            link(V.tensor_scalar(source, source, float(-P), 0.0, ALU.add, ALU.max))

            def take_source(r, i):
                wait(dve, S["xT_ready"], i - XR + 1)
                V.tensor_copy(gidx[r], source[:, bass.ds(2 * i, 2)]).then_inc(S["meta_ready"], 1)

            def take_result(r, i, g):
                wait(dve, s2["y_scattered"][r], 32 * g)
                V.tensor_copy(sidx[r], result[:, bass.ds(2 * i, 2)])

            def x_low(r, i):
                dve.wait_ge(S["xhi_ready"], i + 1)
                V.scalar_tensor_tensor(xT[r % 2][1], banks[2][:, 0:TW], SX, xT[r % 2][0], ALU.mult, ALU.subtract
                                       ).then_inc(S["xlo_ready"], 1)

            def h_mul(h, i):
                dve.wait_ge(S["silu_done"], 2 * i + h + 1)
                wait(dve, S["down_done"], 2 * i + h - 1)
                V.scalar_tensor_tensor(hh[h], banks[h][:, 512:1024], 1.0 / (SX * SW), sg[h],
                                       ALU.mult, ALU.mult).then_inc(S["h_ready"], 1)

            for i in range(AHEAD):
                take_source(i, i)
            link(V.scalar_tensor_tensor(spare_row, result, 0.5, spare_row, ALU.is_lt, ALU.mult))
            link(V.tensor_tensor(result, result, spare_row, ALU.add))
            link(V.tensor_scalar(result, result, float(-P), None, ALU.add))
            x_low(0, 0)

            def expert(g):
                peeled = isinstance(g, int)
                for r in range(XR):
                    i = XR * g + r
                    take_result(r, i, g)
                    if not (peeled and i + AHEAD >= ET):
                        take_source((r + AHEAD) % XR, i + AHEAD)
                    if not (peeled and i + 1 >= ET):
                        x_low((r + 1) % XR, i + 1)
                    h_mul(0, i)
                    h_mul(1, i)

            loop(dve, 0, ET // XR, expert, True)

            def add_up(k):
                dve.wait_ge(s2["yg_loaded"][k % 4], 32 * (k // 4 + 1))
                dve.wait_ge(S["y1_ready"], 2 * k + 2)
                for t in range(YT * k, YT * (k + 1)):
                    last = V.scalar_tensor_tensor(z_all[:, t, :], yg[k % 4][0][:, t % YT, :], gatew[:, t:t + 1],
                                                  yg[k % 4][1][:, t % YT, :], ALU.mult, ALU.add)
                last.then_inc(S["z_ready"], 1)
                dve.wait_ge(S["z_ready"], k + 1)
                for t in range(YT * k, YT * (k + 1)):
                    last = V.bn_stats(stats[:, t, :], z_all[:, t, :])
                link(last)
                moments(k, YT, "z_stats")

            for k in range(NT // YT):
                add_up(k)
                if k:
                    norm(k - 1, YT, "sd2_ready")
            norm(NT // YT - 1, YT, "sd2_ready")


def launch_arrays(x, Wq, bq, Wk, bk, Wv, bv, Wo, bo, phase, threshold, temperature, wg, bg, Wgate, Wup, Wdown):
    f = np.float32
    c = np.ascontiguousarray
    p = (np.arange(L, dtype=f) / f(L) * f(TWO_PI)).astype(f).reshape(8, 64)
    half = p * f(0.5)
    pos = np.stack([p, p, half, np.cos(half.astype(np.float64)).astype(f), np.sin(half.astype(np.float64)).astype(f)], 1)
    pos = np.tile(pos, (NH, 1, 1))
    sel = np.zeros((P, B, P), f)
    for h in range(NH):
        for b in range(B):
            sel[h * B + b, b, h * HD:(h + 1) * HD] = 1
    empty = (2 * T + P + P * np.arange(EB)[None, :] + np.arange(P)[:, None]).astype(f)
    return {
        "xT": c(x.reshape(T, H).T), "x_tok": c(x.reshape(T, H)),
        "W": c(np.stack([Wq, Wk, Wv, Wo], 1)),
        "rows": c(np.concatenate([bv, bo, bg, threshold.reshape(1), temperature.reshape(1)])),
        "ipack": c(np.concatenate([np.repeat(phase, 8, axis=0), bq[:, None], bk[:, None], wg.T], 1)),
        "Wgate": c(Wgate.transpose(2, 0, 1).reshape(P, NE * HID)),
        "Wup": c(Wup.transpose(2, 0, 1).reshape(P, NE * HID)),
        "Wdown": c(Wdown.transpose(2, 0, 1).reshape(4, P, NE, H).transpose(1, 2, 0, 3).reshape(P, NE * HID)),
        "c_sel": sel,
        "cpack": c(np.concatenate([np.eye(P, dtype=f), np.triu(np.ones((P, P), f), 1), pos.reshape(P, 5 * 64),
                                   np.tile(np.arange(NE, dtype=f), (P, 1)), np.tile(np.arange(EB, dtype=f), (P, 1))],
                                  1)),
        "c_route": c(np.concatenate([np.tile(np.arange(P, dtype=f), (P, 1)), empty,
                                     np.tile(np.arange(1, 2 * NT + 1, dtype=f), (P, 1)),
                                     np.arange(P, dtype=f)[:, None]], 1)),
    }


def kernel(**inputs):
    import concourse.bacc as bacc
    from concourse.bass_utils import run_bass_kernel_spmd

    given = {k.split("_", 2)[2]: np.asarray(v) for k, v in inputs.items()}
    arrays = launch_arrays(**given)
    nc = bacc.Bacc("TRN2", target_bir_lowering=False, num_devices=1)
    feeds, aps = {}, {}
    for name, arr in arrays.items():
        feeds[f"in_{name}"] = arr
        aps[name] = nc.dram_tensor(f"in_{name}", arr.shape, mybir.dt.from_np(arr.dtype), kind="ExternalInput").ap()
    out = nc.dram_tensor("out", (T, H), F32, kind="ExternalOutput").ap()
    build(nc, aps, out)
    r = run_bass_kernel_spmd(nc, [feeds], core_ids=[0])
    return r.results[0]["out"].reshape(B, L, H)
```
